# Optimizing a Trainium2 kernel written in Bass

```python
import numpy as np
import jax
import jax.numpy as jnp

def _softmax(x, axis=-1):
    return jax.nn.softmax(x, axis=axis)

def _gelu(x):
    return jax.nn.gelu(x, approximate=True)

def _silu(x):
    return jax.nn.silu(x)

def _sigmoid(x):
    return jax.nn.sigmoid(x)

def _layernorm(x, axis=-1, eps=1e-05):
    m = jnp.mean(x, axis=axis, keepdims=True)
    v = jnp.var(x, axis=axis, keepdims=True)
    return (x - m) / jnp.sqrt(v + eps)

def _scatter_add(tgt, idx, src, axis=0):
    return tgt.at[idx].add(src)

def _segment_sum(src, seg, n):
    return jax.ops.segment_sum(src, seg, n)
kernel_name = 'mk_adj_preln_d2_adj_r2_cf3e8b'

def setup_inputs(seed: int=0):
    np.random.seed(seed)
    _w = jnp.asarray

    def _rec_inputs():
        import jax
        import jax.numpy as jnp
        _gk = jax.random.key(seed)
        x = -0.000125 + 0.9999 * jax.random.normal(jax.random.fold_in(_gk, 1), (32, 256, 128), jnp.float32)
        _w = (1.0 + jnp.arange(256, dtype=jnp.float32)) ** (-0.5)
        _w = _w / _w.mean()
        _pij = jnp.clip(0.0078125 * _w[:, None] * _w[None, :], 0.0, 1.0)
        _a = jax.random.uniform(jax.random.fold_in(_gk, 2), (256, 256)) < _pij
        _a = jnp.logical_or(_a, jnp.swapaxes(_a, -1, -2))
        _a = jnp.logical_or(_a, jnp.eye(256, dtype=bool))
        _af = _a.astype(jnp.float32)
        _af = _af * jax.random.uniform(jax.random.fold_in(_gk, 3), (256, 256), jnp.float32, 0.05, 0.000488281)
        adj = _af
        return (x, adj)
    x, adj = _rec_inputs()

    def _L0_gnn_setup():
        import jax, jax.numpy as jnp
        import numpy as np
        B, T, D, H = (64, 1024, 128, 128)
        MAX_SKIP = 4

        def _lstm_last(Wih, Whh, bih, bhh, xs):
            N, _, Hd = xs.shape
            bias = bih + bhh

            def step(carry, x_t):
                h, c = carry
                g = x_t @ Wih.T + h @ Whh.T + bias
                i, f, gg, o = jnp.split(g, 4, axis=-1)
                c = jax.nn.sigmoid(f) * c + jax.nn.sigmoid(i) * jnp.tanh(gg)
                h = jax.nn.sigmoid(o) * jnp.tanh(c)
                return ((h, c), None)
            init = (jnp.zeros((N, Hd), xs.dtype), jnp.zeros((N, Hd), xs.dtype))
            (h_last, _), _ = jax.lax.scan(step, init, jnp.swapaxes(xs, 0, 1))
            return h_last
        key = jax.random.key(seed)
        ks = jax.random.split(key, 8)
        s = 0.05
        x = jax.random.normal(ks[0], (B, T, D), jnp.float32)
        adj = jax.random.uniform(ks[1], (T, T), jnp.float32) / T
        Wg0 = jax.random.normal(ks[2], (D, H), jnp.float32) * s
        bg0 = jnp.zeros((H,), jnp.float32)
        Wg1 = jax.random.normal(ks[3], (H, H), jnp.float32) * s
        bg1 = jnp.zeros((H,), jnp.float32)
        Wih = jax.random.normal(ks[4], (MAX_SKIP, 4 * H, H), jnp.float32) * s
        Whh = jax.random.normal(ks[5], (MAX_SKIP, 4 * H, H), jnp.float32) * s
        bih = jax.random.normal(ks[6], (MAX_SKIP, 4 * H), jnp.float32) * s
        bhh = jax.random.normal(ks[7], (MAX_SKIP, 4 * H), jnp.float32) * s
        return dict(x=x, adj=adj, Wg0=Wg0, bg0=bg0, Wg1=Wg1, bg1=bg1, Wih=Wih, Whh=Whh, bih=bih, bhh=bhh)
    _L0_gnn_all = _L0_gnn_setup()
    _L0_gnn_in = {k: v for k, v in _L0_gnn_all.items() if k in ('Wg0', 'bg0', 'Wg1', 'bg1', 'Wih', 'Whh', 'bih', 'bhh')}
    del _L0_gnn_all

    def _L1_gnn_setup():
        import jax, jax.numpy as jnp
        import numpy as np
        B, N, IN_DIM, OUT_DIM, H = (2, 2048, 128, 128, 4)
        HEAD_DIM = OUT_DIM // H
        EDGE_P = 0.01
        key = jax.random.key(seed)
        k1, k2, k3 = jax.random.split(key, 3)
        h = jax.random.normal(k1, (B, N, IN_DIM), dtype=jnp.float32)
        W = jax.random.normal(k2, (IN_DIM, 3 * OUT_DIM), dtype=jnp.float32) / np.sqrt(IN_DIM)
        adj = (jax.random.uniform(k3, (N, N)) < EDGE_P).astype(jnp.float32)
        adj = jnp.maximum(adj, jnp.eye(N, dtype=jnp.float32))
        return {'h': h, 'W': W, 'adj': adj}
    _L1_gnn_all = _L1_gnn_setup()
    _L1_gnn_in = {k: v for k, v in _L1_gnn_all.items() if k in ('W',)}
    del _L1_gnn_all
    return {'x': x, 'adj': adj, 'L0_gnn_Wg0': _L0_gnn_in['Wg0'], 'L0_gnn_bg0': _L0_gnn_in['bg0'], 'L0_gnn_Wg1': _L0_gnn_in['Wg1'], 'L0_gnn_bg1': _L0_gnn_in['bg1'], 'L0_gnn_Wih': _L0_gnn_in['Wih'], 'L0_gnn_Whh': _L0_gnn_in['Whh'], 'L0_gnn_bih': _L0_gnn_in['bih'], 'L0_gnn_bhh': _L0_gnn_in['bhh'], 'L1_gnn_W': _L1_gnn_in['W']}

def reference(x, adj, L0_gnn_Wg0, L0_gnn_bg0, L0_gnn_Wg1, L0_gnn_bg1, L0_gnn_Wih, L0_gnn_Whh, L0_gnn_bih, L0_gnn_bhh, L1_gnn_W):
    import jax
    import jax.numpy as jnp

    def _L0_gnn_ref(x, adj, Wg0, bg0, Wg1, bg1, Wih, Whh, bih, bhh):
        import jax, jax.numpy as jnp
        import numpy as np
        B, T, D, H = (64, 1024, 128, 128)
        MAX_SKIP = 4

        def _lstm_last(Wih, Whh, bih, bhh, xs):
            N, _, Hd = xs.shape
            bias = bih + bhh

            def step(carry, x_t):
                h, c = carry
                g = x_t @ Wih.T + h @ Whh.T + bias
                i, f, gg, o = jnp.split(g, 4, axis=-1)
                c = jax.nn.sigmoid(f) * c + jax.nn.sigmoid(i) * jnp.tanh(gg)
                h = jax.nn.sigmoid(o) * jnp.tanh(c)
                return ((h, c), None)
            init = (jnp.zeros((N, Hd), xs.dtype), jnp.zeros((N, Hd), xs.dtype))
            (h_last, _), _ = jax.lax.scan(step, init, jnp.swapaxes(xs, 0, 1))
            return h_last
        h = jax.nn.relu(jnp.einsum('ts,bsh->bth', adj, x @ Wg0 + bg0))
        h = jax.nn.relu(jnp.einsum('ts,bsh->bth', adj, h @ Wg1 + bg1))
        Bv, Tv, Hd = h.shape
        for p in range(1, MAX_SKIP + 1):
            nw = Tv // p
            wins = h[:, :nw * p, :].reshape(Bv * nw, p, Hd)
            last = _lstm_last(Wih[p - 1], Whh[p - 1], bih[p - 1], bhh[p - 1], wins)
            idx = jnp.arange(nw) * p + (p - 1)
            h = h.at[:, idx, :].set(last.reshape(Bv, nw, Hd))
        return h

    def _L1_gnn_ref(h, W, adj):
        import jax, jax.numpy as jnp
        import numpy as np
        B, N, IN_DIM, OUT_DIM, H = (2, 2048, 128, 128, 4)
        HEAD_DIM = OUT_DIM // H
        EDGE_P = 0.01
        Bn, Nn, _ = h.shape
        qkv = h @ W
        qkv = qkv.reshape(Bn, Nn, 3, H, HEAD_DIM).transpose(2, 0, 3, 1, 4)
        q, k, v = (qkv[0], qkv[1], qkv[2])
        mask = jnp.where(adj == 0, -jnp.inf, 0.0)
        scores = jnp.einsum('bhid,bhjd->bhij', q, k) / np.sqrt(HEAD_DIM) + mask
        attn = jax.nn.softmax(scores, axis=-1)
        out = jnp.einsum('bhij,bhjd->bhid', attn, v)
        return out.transpose(0, 2, 1, 3).reshape(Bn, Nn, OUT_DIM)
    h = jnp.maximum(_layernorm(x, axis=-1), 0.0)
    x = x + _L0_gnn_ref(h, adj, L0_gnn_Wg0, L0_gnn_bg0, L0_gnn_Wg1, L0_gnn_bg1, L0_gnn_Wih, L0_gnn_Whh, L0_gnn_bih, L0_gnn_bhh)
    h = jnp.maximum(_layernorm(x, axis=-1), 0.0)
    x = x + _L1_gnn_ref(h, L1_gnn_W, adj)
    return x

_drawn_inputs = setup_inputs


def setup_inputs(seed=0):
    import zlib

    import numpy as np

    out = dict(_drawn_inputs(seed))
    spreads = {'L0_gnn_bg0': (0.0, 0.8), 'L0_gnn_bg1': (0.0, 0.8)}
    factors = {'L0_gnn_Wg0': 8.0,
     'L0_gnn_Wg1': 8.0,
     'L0_gnn_Wih': 8.0,
     'L0_gnn_Whh': 8.0,
     'L0_gnn_bih': 2.946,
     'L0_gnn_bhh': 3.048}
    for name, (base, spread) in spreads.items():
        noise = np.random.default_rng([zlib.crc32(name.encode()), seed]).standard_normal(out[name].shape)
        drawn = base * np.exp(spread * noise) if base else spread * noise
        out[name] = jnp.asarray(drawn.astype(out[name].dtype))
    for name, factor in factors.items():
        out[name] = (out[name] * factor).astype(out[name].dtype)
    return out
```

```python
from contextlib import ExitStack

import concourse.bass as bass
from concourse import mybir

P = 128
B, T, D = 32, 256, 128
GB = 4
NG = B // GB
NT = GB * T // P
COLS = GB * T
HALF = COLS // 2
BANK = 512
HEADS, HD = 4, 32
MAX_SKIP = 4
EPS = 1e-5
MASKED = -1e30

F32 = mybir.dt.float32
F32R = mybir.dt.float32r
ALU = mybir.AluOpType
ACT = mybir.ActivationFunctionType
AX_X = mybir.AxisListType.X

GATE_I, GATE_G, GATE_F, GATE_O = range(4)
REF_BLOCK = {GATE_I: 0, GATE_F: 1, GATE_G: 2, GATE_O: 3}

STEPS = [(1, 0, HALF), (1, 0, HALF)]
STEPS += [(p, k, GB * (T // p)) for p in range(2, MAX_SKIP + 1) for k in range(p)]
NS = len(STEPS)


def gates_of(s):
    return (GATE_I, GATE_G, GATE_O) if STEPS[s][1] == 0 else (GATE_I, GATE_G, GATE_F, GATE_O)


GATE_NO = {}
for _s in range(NS):
    for _gate in gates_of(_s):
        GATE_NO[_s, _gate] = len(GATE_NO) + 1
GATES_PER_GROUP = len(GATE_NO)
UV_NO = {s: 2 * n for n, s in enumerate(s for s in range(NS) if STEPS[s][1])}
UV_PER_GROUP = 2 * len(UV_NO)

NPART = 2 * NT
STACK_DMAS = 2 * 4 * HEADS
LAST_POS = NPART + 2

SCHEDULE = [
    ("x", 0), ("cell", 0), ("L1a",), ("T1",), ("x", 1), ("cell", 1), ("L2a",),
    ("x", 2), ("cell", 2), ("L2b",), ("L1b",),
    ("x", 3), ("T2",), ("h", 3, 0), ("Q",), ("h", 3, 1), ("cell", 3), ("L1c",),
    ("K",), ("x", 4), ("cell", 4), ("G1",), ("pos", 0),
    ("x", 5), ("V",), ("pos", 1), ("h", 5, 0), ("pos", 2), ("h", 5, 1), ("cell", 5), ("pos", 3),
    ("G2",), ("x", 6), ("pos", 4), ("h", 6, 0), ("pos", 5), ("h", 6, 1), ("cell", 6), ("pos", 6),
    ("x", 7), ("cell", 7), ("G3",), ("pos", 7),
    ("x", 8), ("pos", 8), ("h", 8, 0), ("pos", 9), ("h", 8, 1), ("cell", 8), ("pos", 10),
    ("x", 9), ("pos", 11), ("h", 9, 0), ("pos", 12), ("h", 9, 1), ("cell", 9), ("pos", 13),
    ("x", 10), ("pos", 14), ("h", 10, 0), ("pos", 15), ("h", 10, 1), ("cell", 10),
    ("pos", 16), ("G4",), ("pos", 17), ("pos", 18),
]


def part_of(stage):
    name = stage[0]
    if name in ("x", "h", "cell"):
        return "lstm"
    return "gcn" if name[0] == "G" or name[:2] == "L1" else "attn"


def stages(parts):
    return [stage for stage in SCHEDULE if part_of(stage) in parts]


def ring_uses(parts):
    uses = {}
    for stage in stages(parts):
        if stage[0] in ("T1", "T2", "Q", "K", "V", "G1", "G2", "G3", "G4"):
            for half in range(2):
                uses[stage[0], half] = len(uses)
        elif stage[0] == "pos" and stage[1] < NPART:
            uses["S", stage[1]] = len(uses)
    return uses


ALL = ("gcn", "lstm", "attn")
GCN_USES, ALL_USES = len(ring_uses(("gcn",))), len(ring_uses(ALL))
ATTN_USES = len(ring_uses(("lstm", "attn")))


def uses_before(it):
    if isinstance(it, int) and it <= 0:
        return GCN_USES * (it + 1)
    if isinstance(it, int) and it == NG:
        return 2 * GCN_USES + ALL_USES * (NG - 2) + ATTN_USES
    return it * ALL_USES + (2 * GCN_USES - ALL_USES)


class Ring:

    def __init__(self, it, parts, full, read):
        self.uses, self.before, self.full, self.read = ring_uses(parts), uses_before(it), full, read
        self.first = isinstance(it, int) and it < 0

    def bank(self, use):
        return self.uses[use] % 2

    def written(self, use):
        return self.full, self.before + (self.uses[use] + 1)

    def half_before(self):
        return self.before // 2 if isinstance(self.before, int) else self.half

    def was_read(self, use):
        n = self.uses[use]
        return self.read[n % 2], self.half_before() + (n // 2 + 1)

    def is_free(self, use):
        n = self.uses[use]
        if self.first and n < 2:
            return None
        return self.read[n % 2], self.half_before() + n // 2

    def before_was_read(self, back):
        return self.read[back % 2], self.half_before()


def make_ring(it, parts, full, read):
    ring = Ring(it, parts, full, read)
    if not isinstance(it, int):
        ring.half = it * (ALL_USES // 2) + (GCN_USES - ALL_USES // 2)
    return ring


def graph_block(nc, x, adj, Wg0, bg0, Wg1, bg1, Wih, Whh, bih, bhh, Wqkv, out):
    with ExitStack() as ctx:
        def sb(name, shape, dt=F32):
            return ctx.enter_context(nc.sbuf_tensor(name, shape, dt))

        def sem(name):
            return ctx.enter_context(nc.semaphore(name))

        ident = sb("ident", [P, P])
        ones = sb("ones", [P, P])
        shared = sb("shared", [P, 4, NT, D])
        wih_nat = shared[:, 0:2].rearrange("p a t d -> p (a t) d")
        whh_nat = shared[:, 2:4].rearrange("p a t d -> p (a t) d")
        xc2, sq2, hn, y = (shared[:, n] for n in range(4))
        wih_t = sb("wih_t", [P, 4 * MAX_SKIP, P])
        whh_t = sb("whh_t", [P, 4 * MAX_SKIP, P])
        bih_rows = sb("bih_rows", [4 * MAX_SKIP, P])
        bhh_rows = sb("bhh_rows", [4 * MAX_SKIP, P])
        gate_bias = sb("gate_bias", [P, MAX_SKIP, 4])
        wg0 = sb("wg0", [D, D])
        wg1 = sb("wg1", [D, D])
        bg0_col = sb("bg0_col", [D, 1])
        bg1_bc = sb("bg1_bc", [P, D])
        wqkv = sb("wqkv", [D, 3 * D])
        adj_nat = sb("adj_nat", [P, 2, T])
        adj_t = sb("adj_t", [P, 2, T])
        neg_mask = sb("neg_mask", [P, 2, T])
        bias0 = sb("bias0", [D, T])
        minus_half = sb("minus_half", [P, NT])
        x_all = sb("x_all", [P, B * T // P, D])

        mean1, sum1, var1, rstd1 = (sb(n, [P, NT]) for n in ("mean1", "sum1", "var1", "rstd1"))
        xc1 = sb("xc1", [P, NT, D])
        sq1 = sb("sq1", [P, NT, D])
        h0_nat = sb("h0_nat", [P, NT, D])
        z_t = sb("z_t", [P, COLS])
        h1_t = sb("h1_t", [P, COLS])
        y1_nat = sb("y1_nat", [P, NT, D])
        h2_t = sb("h2_t", [P, COLS])

        h_t = sb("h_t", [P, COLS])
        gate = sb("gate", [P, 2, 4, BANK])
        c2, u, v, tanh_c, h_step = (sb(n, [P, BANK]) for n in ("c2", "u", "v", "tanh_c", "h_step"))

        x2 = sb("x2", [P, NT, D])
        mean2, sum2, var2, rstd2 = (sb(n, [P, NT]) for n in ("mean2", "sum2", "var2", "rstd2"))
        hn_t = sb("hn_t", [P, COLS])
        q_hi, q_lo, k_hi, k_lo = (sb(n, [P, COLS], F32R) for n in ("q_hi", "q_lo", "k_hi", "k_lo"))
        q_stack = sb("q_stack", [P, HEADS, COLS], F32R)
        k_stack = sb("k_stack", [P, HEADS, COLS], F32R)
        v_nat = sb("v_nat", [P, NT, D])
        masked = sb("masked", [P, 2, 2, T])
        neg_max = sb("neg_max", [P, 2 * NPART])
        probs = sb("probs", [P, 2, 2, T])
        prob_sum = sb("prob_sum", [P, 2 * NPART])
        prob_rec = sb("prob_rec", [P, NPART])
        probs_t = sb("probs_t", [P, 2, BANK])

        gate_ps = ctx.enter_context(nc.psum_tensor("gate_ps", [P, 4, BANK], F32))
        work_ps = ctx.enter_context(nc.psum_tensor("work_ps", [P, 2, BANK], F32))
        pt_ps = ctx.enter_context(nc.psum_tensor("pt_ps", [P, BANK], F32))
        av_ps = ctx.enter_context(nc.psum_tensor("av_ps", [P, BANK], F32))

        adj_loaded, wih_loaded, whh_loaded = sem("adj_loaded"), sem("wih_loaded"), sem("whh_loaded")
        lstm_bias_loaded, small_loaded = sem("lstm_bias_loaded"), sem("small_loaded")
        x0_loaded, x_loaded = sem("x0_loaded"), sem("x_loaded")
        zeroed, ident_ready, ones_ready, set_up_t, set_up_act, set_up_dve = (
            sem(n) for n in ("zeroed", "ident_ready", "ones_ready", "set_up_t", "set_up_act", "set_up_dve"))
        work_full = sem("work_full")
        work_read = [sem("work_read0"), sem("work_read1")]
        ln1_step, mean1_ready, xc1_ready, sq1_ready, var1_ready, rstd1_ready, h0_ready = (
            sem(n) for n in ("ln1_step", "mean1_ready", "xc1_ready", "sq1_ready", "var1_ready",
                             "rstd1_ready", "h0_ready"))
        x2_ready, ln2_step, var2_ready, rstd2_ready, hn_ready = (
            sem(n) for n in ("x2_ready", "ln2_step", "var2_ready", "rstd2_ready", "hn_ready"))
        h1_ready = sem("h1_ready")
        gate_full, gate_ready, uv_ready, c_ready, tanh_c_ready, h_ready = (
            sem(n) for n in ("gate_full", "gate_ready", "uv_ready", "c_ready", "tanh_c_ready", "h_ready"))
        q_hi_ready, k_hi_ready, stacked = (sem(n) for n in ("q_hi_ready", "k_hi_ready", "stacked"))
        masked_ready, max_ready, exp_ready, pt_full, pt_read, av_done, rec_ready, av_read, y_ready, stored = (
            sem(n) for n in ("masked_ready", "max_ready", "exp_ready", "pt_full", "pt_read", "av_done",
                             "rec_ready", "av_read", "y_ready", "stored"))

        def ring_of(it, parts):
            return make_ring(it, parts, work_full, work_read)

        def window(t, s):
            p, k, n = STEPS[s]
            if p == 1:
                return t[:, s * HALF:(s + 1) * HALF]
            nw = T // p
            return t[:].rearrange("f (b t) -> f b t", b=GB)[:, :, k:k + (nw - 1) * p + 1:p]

        def as_window(ap, s):
            p, _, n = STEPS[s]
            return ap if p == 1 else ap.rearrange("f (b w) -> f b w", b=GB)

        def run(eng, iteration):
            iteration(-1, ("gcn",))
            iteration(0, ("gcn", "lstm"))
            with eng.Fori(1, NG - 1) as it:
                iteration(it, ALL)
            iteration(NG - 1, ("lstm", "attn"))
            iteration(NG, ("attn",))

        block = ctx.enter_context(nc.Block())

        @block.sync
        def _(sp):
            sp.dma_start(adj_nat[:], adj.rearrange("(t p) s -> p t s", p=P)).then_inc(adj_loaded, 16)
            x_tiles = x.rearrange("b (h p) d -> p (b h) d", p=P)
            sp.dma_start(x_all[:, 0:NT, :], x_tiles[:, 0:NT, :]).then_inc(x0_loaded, 16)
            sp.dma_start(wih_nat[:], Wih.rearrange("l (g p) d -> p (l g) d", p=P)).then_inc(wih_loaded, 16)
            sp.dma_start(whh_nat[:], Whh.rearrange("l (g p) d -> p (l g) d", p=P)).then_inc(whh_loaded, 16)
            sp.dma_start(x_all[:, NT:, :], x_tiles[:, NT:, :]).then_inc(x_loaded, 16)
            out_tiles = out.rearrange("b (h p) d -> p (b h) d", p=P)

            sp.sem_inc(stored, 16)

            def iteration(it, parts):
                if "attn" not in parts:
                    return
                ring = ring_of(it, parts)
                for use, hi, lo, stack, quadrants in (("Q", q_hi, q_lo, q_stack, (0, 0, 1, 1)),
                                                      ("K", k_hi, k_lo, k_stack, (0, 1, 0, 1))):
                    sp.wait_ge(*ring.was_read((use, 0)))
                    sp.wait_ge(*ring.was_read((use, 1)))
                    for quadrant, part in enumerate(quadrants):
                        for head in range(HEADS):
                            sp.dma_start(stack[quadrant * HD:(quadrant + 1) * HD, head, :].bitcast(F32),
                                         (hi, lo)[part][head * HD:(head + 1) * HD, :].bitcast(F32)).then_inc(stacked, 16)
                sp.wait_ge(y_ready, it * 2)
                sp.dma_start(out_tiles[:, bass.ds((it - 1) * NT, NT), :], y[:]).then_inc(stored, 16)

            run(sp, iteration)
            sp.wait_ge(stored, 16 * (NG + 1))

        @block.gpsimd
        def _(pool):
            nc.gpsimd.memset(ident[:], 0.0).then_inc(zeroed, 1)
            nc.gpsimd.memset(ones[:], 1.0).then_inc(ones_ready, 1)
            nc.gpsimd.memset(minus_half[:], -0.5).then_inc(zeroed, 1)
            pool.wait_ge(zeroed, 2)
            nc.gpsimd.affine_select(out=ident[:], in_=ident[:], compare_op=ALU.not_equal, fill=1.0, base=0,
                                    pattern=[[-1, P]], channel_multiplier=1).then_inc(ident_ready, 1)

            def iteration(it, parts):
                for stage in stages(parts):
                    if stage[0] == "L1a":
                        g = it + 1
                        rows = x_all[:, bass.ds(g * NT, NT), :]
                        pool.wait_ge(mean1_ready, g + 1)
                        nc.gpsimd.tensor_tensor(xc1[:], rows, mean1[:].unsqueeze(2).to_broadcast([P, NT, D]),
                                                ALU.subtract).then_inc(xc1_ready, 1)
                        pool.wait_ge(xc1_ready, g + 1)
                        nc.gpsimd.tensor_tensor(sq1[:], xc1[:], xc1[:], ALU.mult).then_inc(sq1_ready, 1)
                    elif stage[0] == "L1b":
                        g = it + 1
                        pool.wait_ge(var1_ready, g + 1)
                        nc.gpsimd.tensor_tensor(rstd1[:], var1[:], minus_half[:], ALU.pow).then_inc(rstd1_ready, 1)
                    elif stage[0] == "L2a":
                        g = it - 1
                        pool.wait_ge(var2_ready, g + 1)
                        nc.gpsimd.tensor_tensor(rstd2[:], var2[:], minus_half[:], ALU.pow).then_inc(rstd2_ready, 1)

            run(pool, iteration)

        @block.tensor
        def _(pe):
            mm = nc.tensor.matmul

            pe.wait_ge(ident_ready, 1)
            pe.wait_ge(adj_loaded, 16)
            for st in range(2):
                for tt in range(2):
                    last = nc.tensor.transpose(av_ps[:, st * T + tt * P:st * T + (tt + 1) * P],
                                               adj_nat[:, tt, st * P:(st + 1) * P], ident[:])
            last.then_inc(set_up_t, 1)
            pe.wait_ge(wih_loaded, 16)
            for p in range(MAX_SKIP):
                for blk in range(4):
                    last = nc.tensor.transpose(gate_ps[:, p, blk * P:(blk + 1) * P], wih_nat[:, 4 * p + blk, :], ident[:])
                last.then_inc(set_up_t, 1)
            pe.wait_ge(whh_loaded, 16)
            for p in range(1, MAX_SKIP):
                dst = work_ps[:, p - 1, :] if p < 3 else pt_ps[:]
                for blk in range(4):
                    last = nc.tensor.transpose(dst[:, blk * P:(blk + 1) * P], whh_nat[:, 4 * p + blk, :], ident[:])
                last.then_inc(set_up_t, 1)
            pe.wait_ge(set_up_dve, 2)
            pe.wait_ge(ones_ready, 1)
            for st in range(2):
                mm(av_ps[:, 0:T], ones[:], adj_t[:, st, :], start=st == 0, stop=st == 1)
            nc.tensor.transpose(av_ps[:, T:T + 4 * MAX_SKIP], bih_rows[:],
                                ident[0:4 * MAX_SKIP, 0:4 * MAX_SKIP]).then_inc(set_up_t, 1)
            pe.wait_ge(set_up_act, 7)
            pe.wait_ge(set_up_dve, 7)

            def iteration(it, parts):
                ring = ring_of(it, parts)

                def claim(use):
                    free = ring.is_free(use)
                    if free is not None:
                        pe.wait_ge(*free)
                    return work_ps[:, ring.bank(use), :]

                def free_gate(s, gate_):
                    for back in range(s - 1, -1, -1):
                        if gate_ in gates_of(back):
                            pe.wait_ge(gate_ready, it * GATES_PER_GROUP + GATE_NO[back, gate_])
                            return
                    if isinstance(it, int) and it == 0:
                        return
                    pe.wait_ge(gate_ready, it * GATES_PER_GROUP + (GATE_NO[NS - 1, gate_] - GATES_PER_GROUP))

                for stage in stages(parts):
                    name = stage[0]
                    if name == "x":
                        s = stage[1]
                        p, k, n = STEPS[s]
                        if p == 1:
                            pe.wait_ge(*ring.before_was_read(2 - s))
                        elif k == 0:
                            pe.wait_ge(h_ready, it * NS + s)
                        src = h2_t if p == 1 else h_t
                        for j in gates_of(s):
                            free_gate(s, j)
                            last = mm(gate_ps[:, j, 0:n], wih_t[:, 4 * (p - 1) + REF_BLOCK[j], :], window(src, s),
                                      start=True, stop=k == 0)
                            if k == 0:
                                last.then_inc(gate_full, 1)
                    elif name == "h":
                        s, part = stage[1:]
                        p, k, n = STEPS[s]
                        pe.wait_ge(h_ready, it * NS + s)
                        for j in gates_of(s)[2 * part:2 * part + 2]:
                            mm(gate_ps[:, j, 0:n], whh_t[:, 4 * (p - 1) + REF_BLOCK[j], :], h_step[:, 0:n],
                               start=False, stop=True).then_inc(gate_full, 1)
                    elif name == "T1":
                        pe.wait_ge(h_ready, it * NS)
                        for half in range(2):
                            dst = claim((name, half))
                            for t in range(4):
                                last = nc.tensor.transpose(dst[:, t * P:(t + 1) * P],
                                                           h_t[:, (4 * half + t) * P:(4 * half + t + 1) * P], ident[:])
                            last.then_inc(work_full, 1)
                    elif name == "T2":
                        pe.wait_ge(hn_ready, it)
                        for half in range(2):
                            dst = claim((name, half))
                            for t in range(4):
                                last = nc.tensor.transpose(dst[:, t * P:(t + 1) * P], hn[:, 4 * half + t, :], ident[:])
                            last.then_inc(work_full, 1)
                    elif name in "QK":
                        for half in range(2):
                            if name == "Q":
                                pe.wait_ge(*ring.was_read(("T2", half)))
                            col = "QK".index(name) * D
                            mm(claim((name, half)), wqkv[:, col:col + D], hn_t[:, half * HALF:(half + 1) * HALF],
                               start=True, stop=True).then_inc(work_full, 1)
                    elif name == "V":
                        for half in range(2):
                            dst = claim((name, half))
                            for t in range(4):
                                last = mm(dst[:, t * D:(t + 1) * D], hn_t[:, (4 * half + t) * P:(4 * half + t + 1) * P],
                                          wqkv[:, 2 * D:3 * D], start=True, stop=True)
                            last.then_inc(work_full, 1)
                    elif name == "pos":
                        pos = stage[1]
                        n = pos - 2
                        if 0 <= n < NPART:
                            pe.wait_ge(exp_ready, (it - 1) * NPART + (n + 1))
                            if n:
                                pe.wait_ge(pt_read, (it - 1) * NPART + n)
                            for hk in range(4):
                                last = nc.tensor.transpose(pt_ps[:, hk * P:(hk + 1) * P],
                                                           probs[:, n % 2, hk // 2, (hk % 2) * P:(hk % 2 + 1) * P], ident[:])
                            last.then_inc(pt_full, 1)
                        n = pos - 3
                        if 0 <= n < NPART:
                            pe.wait_ge(pt_read, (it - 1) * NPART + (n + 1))
                            if n == 0:
                                pe.wait_ge(*ring.was_read(("V", 0)))
                                pe.wait_ge(*ring.was_read(("V", 1)))
                            if n == NPART // 2:
                                pe.wait_ge(av_read, (it - 1) * 2 + 1)
                            for hh in range(2):
                                head, col = 2 * (n % 2) + hh, (n % (NPART // 2)) * 2 * HD + hh * HD
                                for kt in range(2):
                                    last = mm(av_ps[:, col:col + HD],
                                              probs_t[:, n % 2, (2 * hh + kt) * P:(2 * hh + kt + 1) * P],
                                              v_nat[:, n // 4 * 2 + kt, head * HD:(head + 1) * HD],
                                              start=kt == 0, stop=kt == 1)
                            last.then_inc(av_done, 1)
                        n = pos
                        if n < NPART:
                            if n == 0:
                                pe.wait_ge(stacked, it * STACK_DMAS * 16)
                            dst = claim(("S", n))
                            for hh in range(2):
                                head = 2 * (n % 2) + hh
                                last = mm(dst[:, hh * T:(hh + 1) * T], q_stack[:, head, n // 2 * P:(n // 2 + 1) * P],
                                          k_stack[:, head, n // 4 * T:(n // 4 + 1) * T], start=True, stop=True)
                            last.then_inc(work_full, 1)
                    elif name in ("G1", "G4"):
                        src = h0_nat if name == "G1" else y1_nat
                        for half in range(2):
                            if name == "G1":
                                pe.wait_ge(h0_ready, it + 2)
                            else:
                                pe.wait_ge(*ring.was_read(("G3", half)))
                            dst = claim((name, half))
                            for b in range(2):
                                for st in range(2):
                                    last = mm(dst[:, b * T:(b + 1) * T], src[:, 4 * half + 2 * b + st, :], adj_t[:, st, :],
                                              start=st == 0, stop=st == 1)
                            last.then_inc(work_full, 1)
                    elif name == "G2":
                        for half in range(2):
                            pe.wait_ge(*ring.was_read(("G1", half)))
                            mm(claim((name, half)), wg0[:], z_t[:, half * HALF:(half + 1) * HALF],
                               start=True, stop=True).then_inc(work_full, 1)
                    elif name == "G3":
                        for half in range(2):
                            pe.wait_ge(h1_ready, (it + 1) * 2 + (half + 1))
                            dst = claim((name, half))
                            for t in range(4):
                                last = mm(dst[:, t * D:(t + 1) * D], h1_t[:, (4 * half + t) * P:(4 * half + t + 1) * P],
                                          wg1[:], start=True, stop=True)
                            last.then_inc(work_full, 1)

            run(pe, iteration)

        @block.scalar
        def _(act):
            act.dma_start(bih_rows[:], bih.rearrange("l (g p) -> (l g) p", p=P)).then_inc(lstm_bias_loaded, 16)
            act.dma_start(bhh_rows[:], bhh.rearrange("l (g p) -> (l g) p", p=P)).then_inc(lstm_bias_loaded, 16)
            act.dma_start(wg0[:], Wg0).then_inc(small_loaded, 16)
            act.dma_start(wg1[:], Wg1).then_inc(small_loaded, 16)
            act.dma_start(wqkv[:], Wqkv).then_inc(small_loaded, 16)
            act.dma_start(bg0_col[:], bg0.rearrange("(p a) -> p a", a=1)).then_inc(small_loaded, 16)
            act.dma_start(bg1_bc[:], bg1.partition_broadcast(P)).then_inc(small_loaded, 16)
            for p in range(MAX_SKIP):
                act.wait_ge(set_up_t, 2 + p)
                nc.scalar.activation(wih_t[:, 4 * p:4 * p + 4, :].rearrange("f g r -> f (g r)"), gate_ps[:, p, :], ACT.Copy,
                                     scale=0.5 if p else 1.0).then_inc(set_up_act, 1)
            for p in range(1, MAX_SKIP):
                act.wait_ge(set_up_t, 5 + p)
                src = work_ps[:, p - 1, :] if p < 3 else pt_ps[:]
                nc.scalar.activation(whh_t[:, 4 * p:4 * p + 4, :].rearrange("f g r -> f (g r)"), src, ACT.Copy,
                                     scale=0.5).then_inc(set_up_act, 1)
            act.wait_ge(set_up_dve, 7)

            def iteration(it, parts):
                ring = ring_of(it, parts)

                def read_work(use, dst, func):
                    act.wait_ge(*ring.written(use))
                    nc.scalar.activation(dst, work_ps[:, ring.bank(use), :], func).then_inc(work_read[ring.bank(use)], 1)

                def gates(s, which):
                    p, k, n = STEPS[s]
                    for j in which:
                        act.wait_ge(gate_full, it * GATES_PER_GROUP + GATE_NO[s, j])
                        nc.scalar.activation(gate[:, s % 2, j, 0:n], gate_ps[:, j, 0:n], ACT.Tanh,
                                             bias=gate_bias[:, p - 1, REF_BLOCK[j]:REF_BLOCK[j] + 1],
                                             scale=1.0 if j == GATE_G else 0.5).then_inc(gate_ready, 1)

                for stage in stages(parts):
                    name = stage[0]
                    if name == "x" and STEPS[stage[1]][1] == 0:
                        s = stage[1]
                        if s == 0 and not (isinstance(it, int) and it == 0):
                            act.wait_ge(h_ready, it * NS)
                        gates(s, gates_of(s))
                    elif name == "h":
                        s, part = stage[1:]
                        gates(s, gates_of(s)[2 * part:2 * part + 2])
                    elif name == "cell":
                        s = stage[1]
                        n = STEPS[s][2]
                        if s == 1:
                            act.wait_ge(h_ready, it * NS + 1)
                        act.wait_ge(c_ready, it * NS + (s + 1))
                        nc.scalar.activation(tanh_c[:, 0:n], c2[:, 0:n], ACT.Tanh, scale=0.5).then_inc(tanh_c_ready, 1)
                    elif name == "T2":
                        for half in range(2):
                            read_work((name, half), hn_t[:, half * HALF:(half + 1) * HALF], ACT.Copy)
                    elif name in ("Q", "K"):
                        for half in range(2):
                            act.wait_ge(*ring.written((name, half)))
                            dst, ready = {"Q": (q_hi, q_hi_ready), "K": (k_hi, k_hi_ready)}[name]
                            nc.scalar.activation(dst[:, half * HALF:(half + 1) * HALF], work_ps[:, ring.bank((name, half)), :],
                                                 ACT.Copy).then_inc(ready, 1)
                    elif name == "V":
                        for half in range(2):
                            read_work((name, half), v_nat[:, 4 * half:4 * half + 4, :].rearrange("p t d -> p (t d)"), ACT.Copy)
                    elif name == "G1":
                        for half in range(2):
                            read_work((name, half), z_t[:, half * HALF:(half + 1) * HALF], ACT.Copy)
                    elif name == "G2":
                        for half in range(2):
                            act.wait_ge(*ring.was_read(("G2", half)))
                            cols = h1_t[:, half * HALF:(half + 1) * HALF]
                            nc.scalar.activation(cols, cols, ACT.Relu).then_inc(h1_ready, 1)
                    elif name == "G4":
                        for half in range(2):
                            read_work((name, half), h2_t[:, half * HALF:(half + 1) * HALF], ACT.Relu)
                    elif name == "pos":
                        n = stage[1] - 1
                        if 0 <= n < NPART:
                            act.wait_ge(max_ready, (it - 1) * NPART + (n + 1))
                            if n >= 2:
                                act.wait_ge(pt_full, (it - 1) * NPART + (n - 1))
                            for hh in range(2):
                                last = nc.scalar.activation(probs[:, n % 2, hh, :], masked[:, n % 2, hh, :], ACT.Exp,
                                                            bias=neg_max[:, 2 * n + hh:2 * n + hh + 1],
                                                            accum_out=prob_sum[:, 2 * n + hh:2 * n + hh + 1])
                            last.then_inc(exp_ready, 1)

            run(act, iteration)

        @block.vector
        def _(dve):
            tt, stt, ts = nc.vector.tensor_tensor, nc.vector.scalar_tensor_tensor, nc.vector.tensor_scalar

            dve.wait_ge(set_up_t, 1)
            nc.vector.tensor_copy(adj_t[:].rearrange("p a t -> p (a t)"), av_ps[:]).then_inc(set_up_dve, 1)
            dve.wait_ge(lstm_bias_loaded, 32)
            tt(bih_rows[:], bih_rows[:], bhh_rows[:], ALU.add).then_inc(set_up_dve, 1)
            ts(neg_mask[:], adj_nat[:], 0.0, MASKED, ALU.is_equal, ALU.mult).then_inc(set_up_dve, 1)
            dve.wait_ge(small_loaded, 80)
            ts(wqkv[:, 0:D], wqkv[:, 0:D], float(HD) ** -0.5, None, ALU.mult).then_inc(set_up_dve, 1)
            dve.wait_ge(set_up_t, 9)
            ts(bias0[:], av_ps[:, 0:T], bg0_col[:, 0:1], None, ALU.mult).then_inc(set_up_dve, 1)
            bias_cols = av_ps[:, T:T + 4 * MAX_SKIP].rearrange("p (l g) -> p l g", g=4)
            ts(gate_bias[:], bias_cols, 0.5, None, ALU.mult).then_inc(set_up_dve, 1)
            dve.wait_ge(set_up_dve, 6)
            g_block = REF_BLOCK[GATE_G]
            ts(gate_bias[:, :, g_block:g_block + 1], bias_cols[:, :, g_block:g_block + 1], 1.0, None,
               ALU.mult).then_inc(set_up_dve, 1)
            dve.wait_ge(x0_loaded, 16)

            def iteration(it, parts):
                ring = ring_of(it, parts)
                if isinstance(it, int) and it == 0:
                    dve.wait_ge(x_loaded, 16)

                def bc(stat):
                    return stat.unsqueeze(2).to_broadcast([P, NT, D])

                def read_two(dst, use, other):
                    dve.wait_ge(*ring.written(use))
                    src = work_ps[:, ring.bank(use), :]
                    if len(other.shape) == 3:
                        src = src.rearrange("p (a b) -> p a b", a=other.shape[1])
                    tt(dst, src, other, ALU.add).then_inc(work_read[ring.bank(use)], 1)

                for stage in stages(parts):
                    name = stage[0]
                    if name == "L1a":
                        g = it + 1
                        rows = x_all[:, bass.ds(g * NT, NT), :]
                        nc.vector.tensor_reduce(sum1[:], rows, axis=AX_X, op=ALU.add).then_inc(ln1_step, 1)
                        dve.wait_ge(ln1_step, g * 2 + 1)
                        ts(mean1[:], sum1[:], 1.0 / D, None, ALU.mult).then_inc(mean1_ready, 1)
                    elif name == "L1b":
                        g = it + 1
                        dve.wait_ge(sq1_ready, g + 1)
                        nc.vector.tensor_reduce(sum1[:], sq1[:], axis=AX_X, op=ALU.add).then_inc(ln1_step, 1)
                        dve.wait_ge(ln1_step, g * 2 + 2)
                        ts(var1[:], sum1[:], 1.0 / D, EPS, ALU.mult, ALU.add).then_inc(var1_ready, 1)
                    elif name == "L1c":
                        g = it + 1
                        dve.wait_ge(rstd1_ready, g + 1)
                        stt(out=h0_nat[:], in0=xc1[:], scalar=0.0, in1=bc(rstd1[:]), op0=ALU.max,
                            op1=ALU.mult).then_inc(h0_ready, 1)
                    elif name == "G2":
                        for half in range(2):
                            read_two(h1_t[:, half * HALF:(half + 1) * HALF].rearrange("f (b t) -> f b t", b=2),
                                     ("G2", half), bias0[:].unsqueeze(1).to_broadcast([D, 2, T]))
                    elif name == "G3":
                        for half in range(2):
                            read_two(y1_nat[:, 4 * half:4 * half + 4, :], ("G3", half),
                                     bg1_bc[:].unsqueeze(1).to_broadcast([P, 4, D]))
                    elif name == "h" and stage[2] == 0:
                        s = stage[1]
                        n = STEPS[s][2]
                        dve.wait_ge(gate_ready, it * GATES_PER_GROUP + GATE_NO[s, GATE_G])
                        stt(out=u[:, 0:n], in0=gate[:, s % 2, GATE_I, 0:n], scalar=1.0, in1=gate[:, s % 2, GATE_G, 0:n],
                            op0=ALU.add, op1=ALU.mult).then_inc(uv_ready, 1)
                    elif name == "cell":
                        s = stage[1]
                        p, k, n = STEPS[s]
                        if k == 0:
                            dve.wait_ge(gate_ready, it * GATES_PER_GROUP + GATE_NO[s, GATE_G])
                            stt(out=c2[:, 0:n], in0=gate[:, s % 2, GATE_I, 0:n], scalar=1.0, in1=gate[:, s % 2, GATE_G, 0:n],
                                op0=ALU.add, op1=ALU.mult).then_inc(c_ready, 1)
                        else:
                            dve.wait_ge(gate_ready, it * GATES_PER_GROUP + GATE_NO[s, GATE_F])
                            stt(out=v[:, 0:n], in0=gate[:, s % 2, GATE_F, 0:n], scalar=1.0, in1=c2[:, 0:n],
                                op0=ALU.add, op1=ALU.mult).then_inc(uv_ready, 1)
                            dve.wait_ge(uv_ready, it * UV_PER_GROUP + (UV_NO[s] + 2))
                            stt(out=c2[:, 0:n], in0=v[:, 0:n], scalar=0.5, in1=u[:, 0:n],
                                op0=ALU.mult, op1=ALU.add).then_inc(c_ready, 1)
                        dve.wait_ge(tanh_c_ready, it * NS + (s + 1))
                        if s == 0 and "attn" in parts:
                            dve.wait_ge(*ring.written(("T1", 1)))
                        dst = window(h_t, s) if k == p - 1 else as_window(h_step[:, 0:n], s)
                        stt(out=dst, in0=as_window(gate[:, s % 2, GATE_O, 0:n], s), scalar=1.0,
                            in1=as_window(tanh_c[:, 0:n], s), op0=ALU.add, op1=ALU.mult).then_inc(h_ready, 1)
                    elif name == "T1":
                        if "lstm" not in parts:
                            dve.wait_ge(y_ready, (it - 1) * 2)
                        for half in range(2):
                            dve.wait_ge(*ring.written((name, half)))
                            stt(out=x2[:, 4 * half:4 * half + 4, :].rearrange("p t d -> p (t d)"),
                                in0=work_ps[:, ring.bank((name, half)), :], scalar=0.5,
                                in1=x_all[:, bass.ds((it - 1) * NT + 4 * half, 4), :].rearrange("p t d -> p (t d)"),
                                op0=ALU.mult, op1=ALU.add).then_inc(work_read[ring.bank((name, half))], 1)
                    elif name == "L2a":
                        g = it - 1
                        step = 0

                        def link(instruction):
                            nonlocal step
                            step += 1
                            instruction.then_inc(ln2_step, 1)
                            dve.wait_ge(ln2_step, g * 5 + step)

                        for half in range(2):
                            dve.wait_ge(*ring.was_read(("T1", half)))
                        link(nc.vector.tensor_reduce(sum2[:], x2[:], axis=AX_X, op=ALU.add))
                        link(ts(mean2[:], sum2[:], 1.0 / D, None, ALU.mult))
                        link(tt(xc2[:], x2[:], bc(mean2[:]), ALU.subtract))
                        link(tt(sq2[:], xc2[:], xc2[:], ALU.mult))
                        link(nc.vector.tensor_reduce(sum2[:], sq2[:], axis=AX_X, op=ALU.add))
                        ts(var2[:], sum2[:], 1.0 / D, EPS, ALU.mult, ALU.add).then_inc(var2_ready, 1)
                    elif name == "L2b":
                        g = it - 1
                        dve.wait_ge(rstd2_ready, g + 1)
                        stt(out=hn[:], in0=xc2[:], scalar=0.0, in1=bc(rstd2[:]), op0=ALU.max,
                            op1=ALU.mult).then_inc(hn_ready, 1)
                    elif name in ("Q", "K"):
                        for half in range(2):
                            hi, lo, hi_ready = {"Q": (q_hi, q_lo, q_hi_ready), "K": (k_hi, k_lo, k_hi_ready)}[name]
                            cols, b = slice(half * HALF, (half + 1) * HALF), ring.bank((name, half))
                            dve.wait_ge(hi_ready, (it - 1) * 2 + (half + 1))
                            tt(lo[:, cols], work_ps[:, b, :], hi[:, cols].bitcast(F32), ALU.subtract).then_inc(work_read[b], 1)
                    elif name == "pos":
                        pos, g = stage[1], it - 1
                        n = pos - 2
                        if 0 <= n < NPART:
                            dve.wait_ge(pt_full, g * NPART + (n + 1))
                            if n >= 2:
                                dve.wait_ge(av_done, g * NPART + (n - 1))
                            nc.vector.tensor_copy(probs_t[:, n % 2, :], pt_ps[:]).then_inc(pt_read, 1)
                        n = pos - 3
                        if n in (NPART // 2 - 1, NPART - 1):
                            r = n // (NPART // 2)
                            dve.wait_ge(exp_ready, g * NPART + (n + 1))
                            nc.vector.reciprocal(prob_rec[:], prob_sum[:, r * NPART:(r + 1) * NPART]).then_inc(rec_ready, 1)
                            dve.wait_ge(rec_ready, g * 2 + (r + 1))
                            dve.wait_ge(av_done, g * NPART + (n + 1))
                            if r == 0:
                                dve.wait_ge(stored, it * 16)
                            ys = y[:, 4 * r:4 * r + 4, :]
                            tt(ys.rearrange("p t (h d) -> p (t h) d", d=HD), av_ps[:].rearrange("p (a d) -> p a d", d=HD),
                               prob_rec[:].unsqueeze(2).to_broadcast([P, NPART, HD]), ALU.mult).then_inc(av_read, 1)
                            dve.wait_ge(av_read, g * 2 + (r + 1))
                            tt(ys, ys, x2[:, 4 * r:4 * r + 4, :], ALU.add).then_inc(y_ready, 1)
                        n = pos
                        if n < NPART:
                            dve.wait_ge(*ring.written(("S", n)))
                            if n >= 2:
                                dve.wait_ge(exp_ready, g * NPART + (n - 1))
                            b = ring.bank(("S", n))
                            tt(masked[:, n % 2, :, :], work_ps[:, b, :].rearrange("p (h j) -> p h j", h=2),
                               neg_mask[:, (n // 2) % 2, :].unsqueeze(1).to_broadcast([P, 2, T]),
                               ALU.add).then_inc(work_read[b], 1)
                            dve.wait_ge(*ring.was_read(("S", n)))
                            nc.vector.tensor_reduce(neg_max[:, 2 * n:2 * n + 2], masked[:, n % 2, :, :], axis=AX_X,
                                                    op=ALU.max, negate=True).then_inc(max_ready, 1)

            run(dve, iteration)


INPUTS = ["x", "adj", "L0_gnn_Wg0", "L0_gnn_bg0", "L0_gnn_Wg1", "L0_gnn_bg1", "L0_gnn_Wih", "L0_gnn_Whh",
          "L0_gnn_bih", "L0_gnn_bhh", "L1_gnn_W"]


def kernel(**inputs):
    import numpy as np
    import concourse.bacc as bacc
    from concourse.bass_utils import run_bass_kernel_spmd

    nc = bacc.Bacc("TRN2", target_bir_lowering=False, num_devices=1)
    arrays, args = {}, []
    for name in INPUTS:
        a = np.ascontiguousarray(inputs[name])
        arrays[f"in_{name}"] = a
        args.append(nc.dram_tensor(f"in_{name}", a.shape, mybir.dt.from_np(a.dtype), kind="ExternalInput").ap())
    args.append(nc.dram_tensor("out", (B, T, D), F32, kind="ExternalOutput").ap())
    graph_block(nc, *args)
    r = run_bass_kernel_spmd(nc, [arrays], core_ids=[0])
    return r.results[0]["out"]
```

```python
from contextlib import ExitStack

import concourse.bass as bass
from concourse import mybir

P = 128
B, T, D = 32, 256, 128
GB = 4
NG = B // GB
NT = GB * T // P
COLS = GB * T
HALF = COLS // 2
BANK = 512
HEADS, HD = 4, 32
MAX_SKIP = 4
EPS = 1e-5
MASKED = 1e30
BIGGEST = 3e38

F32 = mybir.dt.float32
F32R = mybir.dt.float32r
ALU = mybir.AluOpType
ACT = mybir.ActivationFunctionType
AX_X = mybir.AxisListType.X

GATE_I, GATE_G, GATE_F, GATE_O = range(4)
REF_BLOCK = {GATE_I: 0, GATE_F: 1, GATE_G: 2, GATE_O: 3}

STEPS = [(1, 0, HALF), (1, 0, HALF)]
STEPS += [(p, k, GB * (T // p)) for p in range(2, MAX_SKIP + 1) for k in range(p)]
NS = len(STEPS)


def gates_of(s):
    return (GATE_I, GATE_G, GATE_O) if STEPS[s][1] == 0 else (GATE_I, GATE_G, GATE_F, GATE_O)


GATE_NO = {}
for _s in range(NS):
    for _gate in gates_of(_s):
        GATE_NO[_s, _gate] = len(GATE_NO) + 1
GATES_PER_GROUP = len(GATE_NO)
UV_NO = {s: 2 * n for n, s in enumerate(s for s in range(NS) if STEPS[s][1])}
UV_PER_GROUP = 2 * len(UV_NO)

NPART = 2 * NT
STACK_DMAS = 2 * 4
SET_UP_DVE = 17

PE_ORDER = [
    ("x", 0, 0), ("x", 0, 1), ("T1", 0), ("T1", 1), ("x", 1, 0), ("x", 1, 1), ("G1", 0), ("G2", 0),
    ("G1", 1), ("x", 2, 0), ("x", 3, 0), ("x", 2, 1), ("G3", 0), ("G2", 1), ("x", 3, 1), ("T2", 0),
    ("G4", 0), ("Q", 0), ("h", 3, 0), ("h", 3, 1), ("T2", 1), ("G3", 1), ("K", 0), ("G4", 1), ("Q", 1),
    ("x", 4, 0), ("x", 4, 1), ("V", 0), ("V", 1), ("x", 5, 0), ("S", 0), ("x", 5, 1), ("h", 5, 0),
    ("S", 1), ("h", 5, 1), ("S", 2), ("PT", 0), ("x", 6, 0), ("K", 1), ("x", 6, 1), ("PT", 1), ("S", 3),
    ("h", 6, 0), ("AV", 0), ("h", 6, 1), ("S", 4), ("S", 5), ("PT", 2), ("AV", 1), ("PT", 3), ("AV", 2),
    ("S", 6), ("PT", 4), ("S", 7), ("AV", 3), ("PT", 5), ("AV", 4), ("x", 7, 0), ("PT", 6), ("x", 7, 1),
    ("AV", 5), ("AV", 6), ("x", 8, 0), ("S", 8), ("PT", 7), ("S", 9), ("x", 8, 1), ("S", 10), ("AV", 7),
    ("h", 8, 0), ("h", 8, 1), ("S", 11), ("x", 9, 0), ("PT", 8), ("x", 9, 1), ("PT", 9), ("S", 12),
    ("AV", 8), ("S", 13), ("PT", 10), ("h", 9, 0), ("h", 9, 1), ("AV", 9), ("S", 14), ("PT", 11),
    ("S", 15), ("AV", 10), ("PT", 12), ("x", 10, 0), ("x", 10, 1), ("AV", 11), ("PT", 13), ("h", 10, 0),
    ("AV", 12), ("h", 10, 1), ("PT", 14), ("AV", 13), ("PT", 15), ("AV", 14), ("AV", 15),
]
ACT_ORDER = [
    ("gates", 0, 0), ("gates", 0, 1), ("gates", 1, 0), ("tanh", 0), ("G1", 0), ("gates", 1, 1),
    ("tanh", 1), ("gates", 2, 0), ("G2", 0), ("G1", 1), ("gates", 2, 1), ("T2", 0), ("tanh", 2),
    ("G2", 1), ("Q", 0), ("G4", 0), ("gates", 3, 0), ("gates", 3, 1), ("T2", 1), ("K", 0), ("tanh", 3),
    ("G4", 1), ("Q", 1), ("gates", 4, 0), ("gates", 4, 1), ("tanh", 4), ("V", 0), ("V", 1), ("exp", 0),
    ("gates", 5, 0), ("gates", 5, 1), ("exp", 1), ("PT", 0), ("tanh", 5), ("K", 1), ("exp", 2),
    ("PT", 1), ("gates", 6, 0), ("exp", 3), ("gates", 6, 1), ("PT", 2), ("exp", 4), ("PT", 3),
    ("exp", 5), ("PT", 4), ("tanh", 6), ("exp", 6), ("PT", 5), ("gates", 7, 0), ("PT", 6),
    ("gates", 7, 1), ("tanh", 7), ("exp", 7), ("PT", 7), ("exp", 8), ("exp", 9), ("gates", 8, 0),
    ("gates", 8, 1), ("PT", 8), ("exp", 10), ("tanh", 8), ("PT", 9), ("exp", 11), ("PT", 10),
    ("gates", 9, 0), ("exp", 12), ("PT", 11), ("gates", 9, 1), ("exp", 13), ("tanh", 9), ("PT", 12),
    ("exp", 14), ("PT", 13), ("gates", 10, 0), ("exp", 15), ("PT", 14), ("gates", 10, 1), ("PT", 15),
    ("tanh", 10),
]
DVE_ORDER = [
    ("T1", 0), ("T1", 1), ("c", 0), ("L2", 0), ("c", 1), ("h", 0), ("L2", 1), ("h", 1), ("L2", 2),
    ("L2", 3), ("G2", 0), ("L2", 4), ("L2", 5), ("c", 2), ("G3", 0), ("L2", 6), ("G2", 1), ("L1", 0),
    ("h", 2), ("Q", 0), ("G4", 0), ("u", 3), ("L1", 1), ("G3", 1), ("c", 3), ("K", 0), ("h", 3),
    ("Q", 1), ("G4", 1), ("c", 4), ("h", 4), ("max", 0), ("max", 1), ("u", 5), ("c", 5), ("max", 2),
    ("h", 5), ("K", 1), ("max", 3), ("max", 4), ("max", 5), ("u", 6), ("c", 6), ("max", 6), ("max", 7),
    ("h", 6), ("c", 7), ("L1", 2), ("h", 7), ("max", 8), ("max", 9), ("max", 10), ("out", 0),
    ("max", 11), ("u", 8), ("c", 8), ("h", 8), ("max", 12), ("max", 13), ("L1", 3), ("max", 14),
    ("u", 9), ("c", 9), ("max", 15), ("h", 9), ("u", 10), ("c", 10), ("L1", 4), ("h", 10), ("out", 1),
]


def part_of(stage):
    name = stage[0]
    if name in ("x", "h", "gates", "u", "c", "tanh", "cell"):
        return "lstm"
    if name == "L1":
        return "ln1"
    return "gcn" if name[0] == "G" else "attn"


def stages(order, parts):
    return [stage for stage in order if part_of(stage) in parts]


def ring_uses(parts):
    uses = {}
    for stage in stages(PE_ORDER, parts):
        if stage[0] in ("T1", "T2", "Q", "K", "V", "G1", "G2", "G3", "G4", "S"):
            uses[stage] = len(uses)
    return uses


ALL = ("ln1", "gcn", "lstm", "attn")
GCN_USES, ALL_USES = len(ring_uses(("gcn",))), len(ring_uses(ALL))
ATTN_USES = len(ring_uses(("lstm", "attn")))


def uses_before(it):
    if isinstance(it, int) and it <= 0:
        return GCN_USES * max(it + 1, 0)
    if isinstance(it, int) and it == NG:
        return 2 * GCN_USES + ALL_USES * (NG - 2) + ATTN_USES
    return it * ALL_USES + (2 * GCN_USES - ALL_USES)


class Ring:

    def __init__(self, it, parts, full, read):
        self.uses, self.before, self.full, self.read = ring_uses(parts), uses_before(it), full, read
        self.first = isinstance(it, int) and it < 0

    def bank(self, use):
        return self.uses[use] % 2

    def written(self, use):
        return self.full, self.before + (self.uses[use] + 1)

    def half_before(self):
        return self.before // 2 if isinstance(self.before, int) else self.half

    def was_read(self, use):
        n = self.uses[use]
        return self.read[n % 2], self.half_before() + (n // 2 + 1)

    def is_free(self, use):
        n = self.uses[use]
        if self.first and n < 2:
            return None
        return self.read[n % 2], self.half_before() + n // 2

    def before_was_read(self, back):
        return self.read[back % 2], self.half_before()


def make_ring(it, parts, full, read):
    ring = Ring(it, parts, full, read)
    if not isinstance(it, int):
        ring.half = it * (ALL_USES // 2) + (GCN_USES - ALL_USES // 2)
    return ring


def graph_block(nc, x, adj, Wg0, bg0, Wg1, bg1, Wih, Whh, bih, bhh, Wqkv, out):
    with ExitStack() as ctx:
        def sb(name, shape, dt=F32):
            return ctx.enter_context(nc.sbuf_tensor(name, shape, dt))

        def sem(name):
            return ctx.enter_context(nc.semaphore(name))

        ident = sb("ident", [P, P])
        ones = sb("ones", [P, P])
        shared = sb("shared", [P, 4, NT, D])
        wih_nat = shared[:, 0:2].rearrange("p a t d -> p (a t) d")
        whh_nat = shared[:, 2:4].rearrange("p a t d -> p (a t) d")
        x2, xc2, hn, y = (shared[:, n] for n in range(4))
        wih_hi, wih_lo = (sb(n, [P, 4 * MAX_SKIP, P], F32R) for n in ("wih_hi", "wih_lo"))
        whh_hi, whh_lo = (sb(n, [P, 4 * (MAX_SKIP - 1), P], F32R) for n in ("whh_hi", "whh_lo"))
        bih_rows = sb("bih_rows", [4 * MAX_SKIP, P])
        bhh_rows = sb("bhh_rows", [4 * MAX_SKIP, P])
        gate_bias = sb("gate_bias", [P, MAX_SKIP, 4])
        wg0 = sb("wg0", [D, D])
        wg1 = sb("wg1", [D, D])
        bg0_col = sb("bg0_col", [D, 1])
        bg1_bc = sb("bg1_bc", [P, D])
        wqkv = sb("wqkv", [D, 3 * D])
        wqk = sb("wqk", [D, 2, D])
        adj_nat = sb("adj_nat", [P, 2, T])
        adj_t = sb("adj_t", [P, 2, T])
        mask = sb("mask", [P, 2, T])
        bias0 = sb("bias0", [D, T])
        minus_half = sb("minus_half", [P, NT])

        mean1, sum1, var1, rstd1 = (sb(n, [P, NT]) for n in ("mean1", "sum1", "var1", "rstd1"))
        x_ln = sb("x_ln", [P, NT, D])
        xc1 = sb("xc1", [P, NT, D])
        h0_nat = sb("h0_nat", [P, NT, D])
        z_t = sb("z_t", [P, COLS])
        h1_t = sb("h1_t", [P, COLS])
        y1_nat = sb("y1_nat", [P, NT, D])
        h2_hi, h2_lo = (sb(n, [P, COLS], F32R) for n in ("h2_hi", "h2_lo"))

        h_t = sb("h_t", [P, COLS])
        h_hi, h_lo = (sb(n, [P, COLS], F32R) for n in ("h_hi", "h_lo"))
        step_hi, step_lo = (sb(n, [P, BANK], F32R) for n in ("step_hi", "step_lo"))
        gate = sb("gate", [P, 2, 4, BANK])
        c2, tanh_c = (sb(n, [P, 2, BANK]) for n in ("c2", "tanh_c"))
        u, v, h_step = (sb(n, [P, BANK]) for n in ("u", "v", "h_step"))

        x_res = sb("x_res", [P, NT, D])
        mean2, sum2, var2, rstd2 = (sb(n, [P, NT]) for n in ("mean2", "sum2", "var2", "rstd2"))
        hn_t = sb("hn_t", [P, COLS])
        q_hi, q_lo, k_hi, k_lo = (sb(n, [P, COLS], F32R) for n in ("q_hi", "q_lo", "k_hi", "k_lo"))
        q_stack = sb("q_stack", [P, HEADS, COLS], F32R)
        k_stack = sb("k_stack", [P, HEADS, COLS], F32R)
        v_nat = sb("v_nat", [P, NT, D])
        masked = sb("masked", [P, 2, 2, T])
        neg_max = sb("neg_max", [P, 2 * NPART])
        wait_carrier = sb("wait_carrier", [P, NPART])
        probs = sb("probs", [P, 2, 2, T])
        prob_sum = sb("prob_sum", [P, 2 * NPART])
        prob_rec = sb("prob_rec", [P, NPART])
        probs_t = sb("probs_t", [P, 2, BANK])

        gate_ps = ctx.enter_context(nc.psum_tensor("gate_ps", [P, 4, BANK], F32))
        work_ps = ctx.enter_context(nc.psum_tensor("work_ps", [P, 2, BANK], F32))
        pt_ps = ctx.enter_context(nc.psum_tensor("pt_ps", [P, BANK], F32))
        av_ps = ctx.enter_context(nc.psum_tensor("av_ps", [P, BANK], F32))

        adj_loaded, wih_loaded, whh_loaded = sem("adj_loaded"), sem("wih_loaded"), sem("whh_loaded")
        lstm_bias_loaded, small_loaded = sem("lstm_bias_loaded"), sem("small_loaded")
        x_ln_loaded, x_res_loaded = sem("x_ln_loaded"), sem("x_res_loaded")
        zeroed, ident_ready, ones_ready, set_up_t, set_up_act, set_up_dve = (
            sem(n) for n in ("zeroed", "ident_ready", "ones_ready", "set_up_t", "set_up_act", "set_up_dve"))
        work_full = sem("work_full")
        work_read = [sem("work_read0"), sem("work_read1")]
        ln1_step, mean1_ready, xc1_ready, sq1_ready, var1_ready, rstd1_ready, h0_ready = (
            sem(n) for n in ("ln1_step", "mean1_ready", "xc1_ready", "sq1_ready", "var1_ready",
                             "rstd1_ready", "h0_ready"))
        x2_ready, ln2_step, var2_ready, rstd2_ready, hn_ready = (
            sem(n) for n in ("x2_ready", "ln2_step", "var2_ready", "rstd2_ready", "hn_ready"))
        h1_ready = sem("h1_ready")
        gate_full, gate_ready, uv_ready, c_ready, tanh_c_ready, h_ready, h_hi_ready, h_lo_ready, h2_hi_ready = (
            sem(n) for n in ("gate_full", "gate_ready", "uv_ready", "c_ready", "tanh_c_ready", "h_ready",
                             "h_hi_ready", "h_lo_ready", "h2_hi_ready"))
        q_hi_ready, k_hi_ready = sem("q_hi_ready"), sem("k_hi_ready")
        stacked = [sem("stacked0"), sem("stacked1")]
        exp_ready, pt_full, pt_read, av_done, rec_ready, av_read, y_ready, stored = (
            sem(n) for n in ("exp_ready", "pt_full", "pt_read", "av_done", "rec_ready", "av_read",
                             "y_ready", "stored"))

        def ring_of(it, parts):
            return make_ring(it, parts, work_full, work_read)

        def window(t, s, order):
            p, k, _ = STEPS[s]
            if p == 1:
                return t[:].rearrange(f"f ({order}) -> f b t", b=GB)[:, s * GB // 2:(s + 1) * GB // 2, :]
            return t[:].rearrange(f"f ({order}) -> f t b", b=GB)[:, k:k + (T // p - 1) * p + 1:p, :]

        def as_window(ap, s):
            if STEPS[s][0] == 1:
                return ap.rearrange("f (b t) -> f b t", t=T)
            return ap.rearrange("f (w b) -> f w b", b=GB)

        def cell_slot(s):
            return 1 if s == 1 else 0

        def run(eng, iteration):
            iteration(-2, ("ln1",))
            iteration(-1, ("ln1", "gcn"))
            iteration(0, ("ln1", "gcn", "lstm"))
            with eng.Fori(1, NG - 2) as it:
                iteration(it, ALL)
            iteration(NG - 2, ("gcn", "lstm", "attn"))
            iteration(NG - 1, ("lstm", "attn"))
            iteration(NG, ("attn",))

        block = ctx.enter_context(nc.Block())

        @block.sync
        def _(sp):
            sp.dma_start(adj_nat[:], adj.rearrange("(t p) s -> p t s", p=P)).then_inc(adj_loaded, 16)
            x_tiles = x.rearrange("b (h p) d -> p (b h) d", p=P)
            sp.dma_start(x_ln[:], x_tiles[:, 0:NT, :]).then_inc(x_ln_loaded, 16)
            sp.dma_start(wih_nat, Wih.rearrange("l (g p) d -> p (l g) d", p=P)).then_inc(wih_loaded, 16)
            sp.dma_start(whh_nat, Whh.rearrange("l (g p) d -> p (l g) d", p=P)).then_inc(whh_loaded, 16)
            out_tiles = out.rearrange("b (h p) d -> p (b h) d", p=P)
            sp.sem_inc(stored, 16)

            def stack_heads(ring, half):
                cols = slice(half * HALF, (half + 1) * HALF)
                for use, hi, lo, stack, quadrants in (("Q", q_hi, q_lo, q_stack, (0, 0, 1, 1)),
                                                      ("K", k_hi, k_lo, k_stack, (0, 1, 0, 1))):
                    sp.wait_ge(*ring.was_read((use, half)))
                    for quadrant, part in enumerate(quadrants):
                        sp.dma_start(stack[quadrant * HD:(quadrant + 1) * HD, :, cols].bitcast(F32),
                                     (hi, lo)[part][:, cols].bitcast(F32)).then_inc(stacked[half], 16)

            def iteration(it, parts):
                if "ln1" in parts and not (isinstance(it, int) and it < -1):
                    sp.wait_ge(xc1_ready, it + 2)
                    sp.dma_start(x_ln[:], x_tiles[:, bass.ds((it + 2) * NT, NT), :]).then_inc(x_ln_loaded, 16)
                if "attn" in parts:
                    stack_heads(ring_of(it, parts), 0)
                    stack_heads(ring_of(it, parts), 1)
                if "lstm" in parts:
                    sp.dma_start(x_res[:], x_tiles[:, bass.ds(it * NT, NT), :]).then_inc(x_res_loaded, 16)
                if "attn" in parts:
                    sp.wait_ge(y_ready, (it + 1) * 2)
                    sp.dma_start(out_tiles[:, bass.ds((it - 1) * NT, NT), :], y).then_inc(stored, 16)

            run(sp, iteration)
            sp.wait_ge(stored, 16 * (NG + 1))

        @block.gpsimd
        def _(pool):
            nc.gpsimd.memset(ident[:], 0.0).then_inc(zeroed, 1)
            nc.gpsimd.memset(ones[:], 1.0).then_inc(ones_ready, 1)
            nc.gpsimd.memset(minus_half[:], -0.5).then_inc(zeroed, 1)
            pool.wait_ge(zeroed, 2)
            nc.gpsimd.affine_select(out=ident[:], in_=ident[:], compare_op=ALU.not_equal, fill=1.0, base=0,
                                    pattern=[[-1, P]], channel_multiplier=1).then_inc(ident_ready, 1)


            def iteration(it, parts):
                ring = ring_of(it, parts)
                if "attn" in parts:
                    pool.wait_ge(var2_ready, it)
                    nc.gpsimd.tensor_tensor(rstd2[:], var2[:], minus_half[:], ALU.pow).then_inc(rstd2_ready, 1)
                if "ln1" in parts:
                    g = it + 2
                    pool.wait_ge(mean1_ready, g + 1)
                    nc.gpsimd.tensor_tensor(xc1[:], x_ln[:], mean1[:].unsqueeze(2).to_broadcast([P, NT, D]),
                                            ALU.subtract).then_inc(xc1_ready, 1)
                    pool.wait_ge(xc1_ready, g + 1)
                    if "gcn" in parts:
                        pool.wait_ge(*ring.written(("G1", 1)))
                    nc.gpsimd.tensor_tensor(h0_nat[:], xc1[:], xc1[:], ALU.mult).then_inc(sq1_ready, 1)
                    pool.wait_ge(var1_ready, g + 1)
                    nc.gpsimd.tensor_tensor(rstd1[:], var1[:], minus_half[:], ALU.pow).then_inc(rstd1_ready, 1)

            run(pool, iteration)

        @block.tensor
        def _(pe):
            mm = nc.tensor.matmul

            pe.wait_ge(ident_ready, 1)
            pe.wait_ge(adj_loaded, 16)
            for st in range(2):
                for tt in range(2):
                    last = nc.tensor.transpose(av_ps[:, st * T + tt * P:st * T + (tt + 1) * P],
                                               adj_nat[:, tt, st * P:(st + 1) * P], ident[:])
            last.then_inc(set_up_t, 1)
            pe.wait_ge(wih_loaded, 16)
            for p in range(MAX_SKIP):
                for blk in range(4):
                    last = nc.tensor.transpose(gate_ps[:, p, blk * P:(blk + 1) * P], wih_nat[:, 4 * p + blk, :], ident[:])
                last.then_inc(set_up_t, 1)
            pe.wait_ge(whh_loaded, 16)
            for p in range(1, MAX_SKIP):
                dst = work_ps[:, p - 1, :] if p < 3 else pt_ps[:]
                for blk in range(4):
                    last = nc.tensor.transpose(dst[:, blk * P:(blk + 1) * P], whh_nat[:, 4 * p + blk, :], ident[:])
                last.then_inc(set_up_t, 1)
            pe.wait_ge(set_up_dve, 2)
            pe.wait_ge(ones_ready, 1)
            for st in range(2):
                mm(av_ps[:, 0:T], ones[:], adj_t[:, st, :], start=st == 0, stop=st == 1)
            nc.tensor.transpose(av_ps[:, T:T + 4 * MAX_SKIP], bih_rows[:],
                                ident[0:4 * MAX_SKIP, 0:4 * MAX_SKIP]).then_inc(set_up_t, 1)
            pe.wait_ge(set_up_act, 7)
            pe.wait_ge(set_up_dve, SET_UP_DVE)

            def iteration(it, parts):
                ring = ring_of(it, parts)

                def claim(use):
                    free = ring.is_free(use)
                    if free is not None:
                        pe.wait_ge(*free)
                    return work_ps[:, ring.bank(use), :]

                def free_gate(s, gate_):
                    for back in range(s - 1, -1, -1):
                        if gate_ in gates_of(back):
                            pe.wait_ge(gate_ready, it * GATES_PER_GROUP + GATE_NO[back, gate_])
                            return
                    if isinstance(it, int) and it == 0:
                        return
                    pe.wait_ge(gate_ready, it * GATES_PER_GROUP + (GATE_NO[NS - 1, gate_] - GATES_PER_GROUP))

                for stage in stages(PE_ORDER, parts):
                    name = stage[0]
                    if name == "x":
                        s, part = stage[1:]
                        p, k, n = STEPS[s]
                        if p == 1:
                            pe.wait_ge(*ring.before_was_read(2 - s))
                        elif k == 0:
                            pe.wait_ge(h_hi_ready, it * NS + s)
                        x_hi, x_lo = (h2_hi[:, s * HALF:(s + 1) * HALF], h2_lo[:, s * HALF:(s + 1) * HALF]) if p == 1 \
                            else (window(h_hi, s, "t b"), window(h_lo, s, "t b"))
                        which = gates_of(s)[2 * part:2 * part + 2]
                        for j in which:
                            free_gate(s, j)
                            blk, dst = 4 * (p - 1) + REF_BLOCK[j], gate_ps[:, j, 0:n]
                            mm(dst, wih_hi[:, blk, :], x_hi, start=True, stop=False)
                            mm(dst, wih_lo[:, blk, :], x_hi, start=False, stop=False)
                        if p > 1 and k == 0:
                            pe.wait_ge(h_lo_ready, it * NS + s)
                        for j in which:
                            blk, dst = 4 * (p - 1) + REF_BLOCK[j], gate_ps[:, j, 0:n]
                            last = mm(dst, wih_hi[:, blk, :], x_lo, start=False, stop=k == 0)
                            if k == 0:
                                last.then_inc(gate_full, 1)
                    elif name == "h":
                        s, part = stage[1:]
                        p, k, n = STEPS[s]
                        which = gates_of(s)[2 * part:2 * part + 2]
                        pe.wait_ge(h_hi_ready, it * NS + s)
                        for j in which:
                            blk, dst = 4 * (p - 2) + REF_BLOCK[j], gate_ps[:, j, 0:n]
                            mm(dst, whh_hi[:, blk, :], step_hi[:, 0:n], start=False, stop=False)
                            mm(dst, whh_lo[:, blk, :], step_hi[:, 0:n], start=False, stop=False)
                        pe.wait_ge(h_lo_ready, it * NS + s)
                        for j in which:
                            blk, dst = 4 * (p - 2) + REF_BLOCK[j], gate_ps[:, j, 0:n]
                            mm(dst, whh_hi[:, blk, :], step_lo[:, 0:n], start=False, stop=True).then_inc(gate_full, 1)
                    elif name in ("T1", "T2"):
                        half = stage[1]
                        if name == "T1":
                            pe.wait_ge(h_ready, it * NS)
                        else:
                            pe.wait_ge(hn_ready, it)
                        dst = claim(stage)
                        for t in range(4 * half, 4 * half + 4):
                            src = h_t[:, t * P:(t + 1) * P] if name == "T1" else hn[:, t, :]
                            last = nc.tensor.transpose(dst[:, t % 4 * P:(t % 4 + 1) * P], src, ident[:])
                        last.then_inc(work_full, 1)
                    elif name in ("Q", "K"):
                        half = stage[1]
                        pe.wait_ge(*ring.was_read(("T2", half)))
                        mm(claim(stage), wqk[:, "QK".index(name), :], hn_t[:, half * HALF:(half + 1) * HALF],
                           start=True, stop=True).then_inc(work_full, 1)
                    elif name == "V":
                        half = stage[1]
                        pe.wait_ge(*ring.was_read(("T2", half)))
                        dst = claim(stage)
                        for t in range(4):
                            last = mm(dst[:, t * D:(t + 1) * D], hn_t[:, (4 * half + t) * P:(4 * half + t + 1) * P],
                                      wqkv[:, 2 * D:3 * D], start=True, stop=True)
                        last.then_inc(work_full, 1)
                    elif name == "S":
                        n = stage[1]
                        dst = claim(stage)
                        if n % (NPART // 2) == 0:
                            pe.wait_ge(stacked[n // (NPART // 2)], it * STACK_DMAS * 16)
                        for hh in range(2):
                            head = 2 * (n % 2) + hh
                            last = mm(dst[:, hh * T:(hh + 1) * T], q_stack[:, head, n // 2 * P:(n // 2 + 1) * P],
                                      k_stack[:, head, n // 4 * T:(n // 4 + 1) * T], start=True, stop=True)
                        last.then_inc(work_full, 1)
                    elif name == "PT":
                        n = stage[1]
                        pe.wait_ge(exp_ready, (it - 1) * NPART + (n + 1))
                        if n:
                            pe.wait_ge(pt_read, (it - 1) * NPART + n)
                        for hk in range(4):
                            last = nc.tensor.transpose(pt_ps[:, hk * P:(hk + 1) * P],
                                                       probs[:, n % 2, hk // 2, (hk % 2) * P:(hk % 2 + 1) * P], ident[:])
                        last.then_inc(pt_full, 1)
                    elif name == "AV":
                        n = stage[1]
                        pe.wait_ge(pt_read, (it - 1) * NPART + (n + 1))
                        if n == 0:
                            pe.wait_ge(*ring.was_read(("V", 1)))
                        if n == NPART // 2:
                            pe.wait_ge(av_read, (it - 1) * 2 + 1)
                        for hh in range(2):
                            head, col = 2 * (n % 2) + hh, (n % (NPART // 2)) * 2 * HD + hh * HD
                            for kt in range(2):
                                last = mm(av_ps[:, col:col + HD],
                                          probs_t[:, n % 2, (2 * hh + kt) * P:(2 * hh + kt + 1) * P],
                                          v_nat[:, n // 4 * 2 + kt, head * HD:(head + 1) * HD],
                                          start=kt == 0, stop=kt == 1)
                        last.then_inc(av_done, 1)
                    elif name in ("G1", "G4"):
                        half = stage[1]
                        if name == "G1":
                            src = h0_nat
                            pe.wait_ge(h0_ready, it + 2)
                        else:
                            src = y1_nat
                            pe.wait_ge(*ring.was_read(("G3", half)))
                        dst = claim(stage)
                        for b in range(2):
                            for st in range(2):
                                last = mm(dst[:, b * T:(b + 1) * T], src[:, 4 * half + 2 * b + st, :], adj_t[:, st, :],
                                          start=st == 0, stop=st == 1)
                        last.then_inc(work_full, 1)
                    elif name == "G2":
                        half = stage[1]
                        pe.wait_ge(*ring.was_read(("G1", half)))
                        mm(claim(stage), wg0[:], z_t[:, half * HALF:(half + 1) * HALF],
                           start=True, stop=True).then_inc(work_full, 1)
                    elif name == "G3":
                        half = stage[1]
                        pe.wait_ge(h1_ready, (it + 1) * 2 + (half + 1))
                        dst = claim(stage)
                        for t in range(4):
                            last = mm(dst[:, t * D:(t + 1) * D], h1_t[:, (4 * half + t) * P:(4 * half + t + 1) * P],
                                      wg1[:], start=True, stop=True)
                        last.then_inc(work_full, 1)

            run(pe, iteration)

        @block.scalar
        def _(act):
            act.dma_start(bih_rows[:], bih.rearrange("l (g p) -> (l g) p", p=P)).then_inc(lstm_bias_loaded, 16)
            act.dma_start(bhh_rows[:], bhh.rearrange("l (g p) -> (l g) p", p=P)).then_inc(lstm_bias_loaded, 16)
            act.dma_start(wg0[:], Wg0).then_inc(small_loaded, 16)
            act.dma_start(wg1[:], Wg1).then_inc(small_loaded, 16)
            act.dma_start(wqkv[:], Wqkv).then_inc(small_loaded, 16)
            act.dma_start(bg0_col[:], bg0.rearrange("(p a) -> p a", a=1)).then_inc(small_loaded, 16)
            act.dma_start(bg1_bc[:], bg1.partition_broadcast(P)).then_inc(small_loaded, 16)
            for p in range(MAX_SKIP):
                act.wait_ge(set_up_t, 2 + p)
                nc.scalar.activation(wih_hi[:, 4 * p:4 * p + 4, :].rearrange("f g r -> f (g r)"), gate_ps[:, p, :], ACT.Copy,
                                     scale=0.5 if p else 1.0).then_inc(set_up_act, 1)
            for p in range(1, MAX_SKIP):
                act.wait_ge(set_up_t, 5 + p)
                src = work_ps[:, p - 1, :] if p < 3 else pt_ps[:]
                nc.scalar.activation(whh_hi[:, 4 * p - 4:4 * p, :].rearrange("f g r -> f (g r)"), src, ACT.Copy,
                                     scale=0.5).then_inc(set_up_act, 1)
            act.wait_ge(set_up_dve, SET_UP_DVE)

            def iteration(it, parts):
                ring = ring_of(it, parts)

                for stage in stages(ACT_ORDER, parts):
                    name = stage[0]
                    if name == "gates":
                        s, part = stage[1:]
                        p, k, n = STEPS[s]
                        if stage == ("gates", 0, 0) and not (isinstance(it, int) and it == 0):
                            act.wait_ge(h_ready, it * NS)
                        for j in gates_of(s)[2 * part:2 * part + 2]:
                            act.wait_ge(gate_full, it * GATES_PER_GROUP + GATE_NO[s, j])
                            nc.scalar.activation(gate[:, s % 2, j, 0:n], gate_ps[:, j, 0:n], ACT.Tanh,
                                                 bias=gate_bias[:, p - 1, REF_BLOCK[j]:REF_BLOCK[j] + 1],
                                                 scale=1.0 if j == GATE_G else 0.5).then_inc(gate_ready, 1)
                    elif name == "tanh":
                        s = stage[1]
                        n = STEPS[s][2]
                        act.wait_ge(c_ready, it * NS + (s + 1))
                        nc.scalar.activation(tanh_c[:, cell_slot(s), 0:n], c2[:, cell_slot(s), 0:n], ACT.Tanh,
                                             scale=0.5).then_inc(tanh_c_ready, 1)
                    elif name == "G2":
                        act.wait_ge(*ring.was_read(stage))
                        half = stage[1]
                        cols = h1_t[:, half * HALF:(half + 1) * HALF]
                        nc.scalar.activation(cols, cols, ACT.Relu).then_inc(h1_ready, 1)
                    elif name in ("Q", "K", "G4"):
                        act.wait_ge(*ring.written(stage))
                        half = stage[1]
                        dst, ready, func = {"Q": (q_hi, q_hi_ready, ACT.Copy), "K": (k_hi, k_hi_ready, ACT.Copy),
                                            "G4": (h2_hi, h2_hi_ready, ACT.Relu)}[name]
                        nc.scalar.activation(dst[:, half * HALF:(half + 1) * HALF], work_ps[:, ring.bank(stage), :],
                                             func).then_inc(ready, 1)
                    elif name in ("T2", "V", "G1"):
                        act.wait_ge(*ring.written(stage))
                        half = stage[1]
                        dst = v_nat[:].rearrange("p t d -> p (t d)") if name == "V" else (hn_t if name == "T2" else z_t)[:]
                        nc.scalar.activation(dst[:, half * HALF:(half + 1) * HALF], work_ps[:, ring.bank(stage), :],
                                             ACT.Copy).then_inc(work_read[ring.bank(stage)], 1)
                    elif name == "exp":
                        n = stage[1]
                        act.wait_ge(*ring.was_read(("S", n)))
                        if n >= 2:
                            act.wait_ge(pt_full, (it - 1) * NPART + (n - 1))
                        for hh in range(2):
                            last = nc.scalar.activation(probs[:, n % 2, hh, :], masked[:, n % 2, hh, :], ACT.Exp,
                                                        scale=-1.0, bias=neg_max[:, 2 * n + hh:2 * n + hh + 1],
                                                        accum_out=prob_sum[:, 2 * n + hh:2 * n + hh + 1])
                        last.then_inc(exp_ready, 1)
                    elif name == "PT":
                        n = stage[1]
                        act.wait_ge(pt_full, (it - 1) * NPART + (n + 1))
                        if n >= 2:
                            act.wait_ge(av_done, (it - 1) * NPART + (n - 1))
                        nc.scalar.activation(probs_t[:, n % 2, :], pt_ps[:], ACT.Copy).then_inc(pt_read, 1)

            run(act, iteration)

        @block.vector
        def _(dve):
            tt, stt, ts = nc.vector.tensor_tensor, nc.vector.scalar_tensor_tensor, nc.vector.tensor_scalar

            def row_sums(g):
                dve.wait_ge(x_ln_loaded, (g + 1) * 16)
                nc.vector.tensor_reduce(sum1[:], x_ln[:], axis=AX_X, op=ALU.add).then_inc(ln1_step, 1)

            def means(g):
                dve.wait_ge(ln1_step, g * 2 + 1)
                ts(mean1[:], sum1[:], 1.0 / D, None, ALU.mult).then_inc(mean1_ready, 1)

            dve.wait_ge(set_up_t, 1)
            nc.vector.tensor_copy(adj_t[:].rearrange("p a t -> p (a t)"), av_ps[:]).then_inc(set_up_dve, 1)
            dve.wait_ge(lstm_bias_loaded, 32)
            tt(bih_rows[:], bih_rows[:], bhh_rows[:], ALU.add).then_inc(set_up_dve, 1)
            ts(mask[:], adj_nat[:], 0.0, MASKED, ALU.is_equal, ALU.mult).then_inc(set_up_dve, 1)
            row_sums(0)
            means(0)
            for p in range(MAX_SKIP):
                dve.wait_ge(set_up_act, 1 + p)
                stt(out=wih_lo[:, 4 * p:4 * p + 4, :].rearrange("f g r -> f (g r)"), in0=gate_ps[:, p, :],
                    scalar=0.5 if p else 1.0, in1=wih_hi[:, 4 * p:4 * p + 4, :].rearrange("f g r -> f (g r)").bitcast(F32),
                    op0=ALU.mult, op1=ALU.subtract).then_inc(set_up_dve, 1)
            for p in range(1, MAX_SKIP):
                dve.wait_ge(set_up_act, 4 + p)
                src = work_ps[:, p - 1, :] if p < 3 else pt_ps[:]
                stt(out=whh_lo[:, 4 * p - 4:4 * p, :].rearrange("f g r -> f (g r)"), in0=src, scalar=0.5,
                    in1=whh_hi[:, 4 * p - 4:4 * p, :].rearrange("f g r -> f (g r)").bitcast(F32),
                    op0=ALU.mult, op1=ALU.subtract).then_inc(set_up_dve, 1)
            dve.wait_ge(set_up_t, 9)
            dve.wait_ge(small_loaded, 80)
            ts(bias0[:], av_ps[:, 0:T], bg0_col[:, 0:1], None, ALU.mult).then_inc(set_up_dve, 1)
            bias_cols = av_ps[:, T:T + 4 * MAX_SKIP].rearrange("p (l g) -> p l g", g=4)
            for blk in range(4):
                ts(gate_bias[:, :, blk:blk + 1], bias_cols[:, :, blk:blk + 1], 1.0 if blk == REF_BLOCK[GATE_G] else 0.5,
                   None, ALU.mult).then_inc(set_up_dve, 1)
            for col, scale in enumerate((-float(HD) ** -0.5, 1.0)):
                ts(wqk[:, col, :].rearrange("f (d h) -> f d h", h=HEADS),
                   wqkv[:, col * D:(col + 1) * D].rearrange("f (h d) -> f d h", h=HEADS), scale, None,
                   ALU.mult).then_inc(set_up_dve, 1)

            dve.sem_inc(y_ready, 2)

            def iteration(it, parts):
                ring = ring_of(it, parts)

                def bc(stat):
                    return stat.unsqueeze(2).to_broadcast([P, NT, D])

                for stage in stages(DVE_ORDER, parts):
                    name = stage[0]
                    if name == "L1":
                        g, step = it + 2, stage[1]
                        if step < 2:
                            if not (isinstance(it, int) and it == -2):
                                (row_sums, means)[step](g)
                        elif step == 2:
                            dve.wait_ge(sq1_ready, g + 1)
                            nc.vector.tensor_reduce(sum1[:], h0_nat[:], axis=AX_X, op=ALU.add).then_inc(ln1_step, 1)
                        elif step == 3:
                            dve.wait_ge(ln1_step, g * 2 + 2)
                            ts(var1[:], sum1[:], 1.0 / D, EPS, ALU.mult, ALU.add).then_inc(var1_ready, 1)
                        else:
                            dve.wait_ge(rstd1_ready, g + 1)
                            stt(out=h0_nat[:], in0=xc1[:], scalar=0.0, in1=bc(rstd1[:]), op0=ALU.max,
                                op1=ALU.mult).then_inc(h0_ready, 1)
                    elif name == "G2":
                        dve.wait_ge(*ring.written(stage))
                        half, bank = stage[1], ring.bank(stage)
                        tt(h1_t[:, half * HALF:(half + 1) * HALF].rearrange("f (b t) -> f b t", b=2),
                           work_ps[:, bank, :].rearrange("f (b t) -> f b t", b=2),
                           bias0[:].unsqueeze(1).to_broadcast([D, 2, T]), ALU.add).then_inc(work_read[bank], 1)
                    elif name == "G3":
                        dve.wait_ge(*ring.written(stage))
                        half, bank = stage[1], ring.bank(stage)
                        tt(y1_nat[:, 4 * half:4 * half + 4, :], work_ps[:, bank, :].rearrange("p (t d) -> p t d", d=D),
                           bg1_bc[:].unsqueeze(1).to_broadcast([P, 4, D]), ALU.add).then_inc(work_read[bank], 1)
                    elif name == "G4":
                        half, bank = stage[1], ring.bank(stage)
                        cols = slice(half * HALF, (half + 1) * HALF)
                        dve.wait_ge(h2_hi_ready, (it + 1) * 2 + (half + 1))
                        stt(out=h2_lo[:, cols], in0=work_ps[:, bank, :], scalar=0.0, in1=h2_hi[:, cols].bitcast(F32),
                            op0=ALU.max, op1=ALU.subtract).then_inc(work_read[bank], 1)
                    elif name == "u":
                        s = stage[1]
                        n = STEPS[s][2]
                        dve.wait_ge(gate_ready, it * GATES_PER_GROUP + GATE_NO[s, GATE_G])
                        stt(out=u[:, 0:n], in0=gate[:, s % 2, GATE_I, 0:n], scalar=1.0, in1=gate[:, s % 2, GATE_G, 0:n],
                            op0=ALU.add, op1=ALU.mult).then_inc(uv_ready, 1)
                    elif name == "c":
                        s = stage[1]
                        p, k, n = STEPS[s]
                        c_now = c2[:, cell_slot(s), 0:n]
                        if k == 0:
                            dve.wait_ge(gate_ready, it * GATES_PER_GROUP + GATE_NO[s, GATE_G])
                            stt(out=c_now, in0=gate[:, s % 2, GATE_I, 0:n], scalar=1.0, in1=gate[:, s % 2, GATE_G, 0:n],
                                op0=ALU.add, op1=ALU.mult).then_inc(c_ready, 1)
                        else:
                            dve.wait_ge(gate_ready, it * GATES_PER_GROUP + GATE_NO[s, GATE_F])
                            stt(out=v[:, 0:n], in0=gate[:, s % 2, GATE_F, 0:n], scalar=1.0, in1=c_now,
                                op0=ALU.add, op1=ALU.mult).then_inc(uv_ready, 1)
                            dve.wait_ge(uv_ready, it * UV_PER_GROUP + (UV_NO[s] + 2))
                            stt(out=c_now, in0=v[:, 0:n], scalar=0.5, in1=u[:, 0:n],
                                op0=ALU.mult, op1=ALU.add).then_inc(c_ready, 1)
                    elif name == "h":
                        s = stage[1]
                        p, k, n = STEPS[s]
                        dve.wait_ge(tanh_c_ready, it * NS + (s + 1))
                        dve.wait_ge(gate_ready, it * GATES_PER_GROUP + GATE_NO[s, GATE_O])
                        if s == 0 and "attn" in parts:
                            dve.wait_ge(*ring.written(("T1", 1)))
                        if k == p - 1:
                            whole, hi, lo = window(h_t, s, "b t"), window(h_hi, s, "t b"), window(h_lo, s, "t b")
                        else:
                            whole, hi, lo = (as_window(t[:, 0:n], s) for t in (h_step, step_hi, step_lo))
                        stt(out=whole, in0=as_window(gate[:, s % 2, GATE_O, 0:n], s), scalar=1.0,
                            in1=as_window(tanh_c[:, cell_slot(s), 0:n], s), op0=ALU.add, op1=ALU.mult).then_inc(h_ready, 1)
                        dve.wait_ge(h_ready, it * NS + (s + 1))
                        nc.vector.tensor_copy(hi, whole).then_inc(h_hi_ready, 1)
                        dve.wait_ge(h_hi_ready, it * NS + (s + 1))
                        tt(lo, whole, hi.bitcast(F32), ALU.subtract).then_inc(h_lo_ready, 1)
                    elif name == "T1":
                        half, bank = stage[1], ring.bank(stage)
                        dve.wait_ge(y_ready, it * 2)
                        dve.wait_ge(x_res_loaded, it * 16)
                        dve.wait_ge(*ring.written(stage))
                        stt(out=x2[:, 4 * half:4 * half + 4, :].rearrange("p t d -> p (t d)"),
                            in0=work_ps[:, bank, :], scalar=0.5,
                            in1=x_res[:, 4 * half:4 * half + 4, :].rearrange("p t d -> p (t d)"),
                            op0=ALU.mult, op1=ALU.add).then_inc(work_read[bank], 1)
                    elif name == "L2":
                        g, step = it - 1, stage[1]
                        if step == 0:
                            dve.wait_ge(*ring.was_read(("T1", 1)))
                            nc.vector.tensor_reduce(sum2[:], x2, axis=AX_X, op=ALU.add).then_inc(ln2_step, 1)
                        elif step <= 5:
                            dve.wait_ge(ln2_step, g * 5 + step)
                        if step == 1:
                            ts(mean2[:], sum2[:], 1.0 / D, None, ALU.mult).then_inc(ln2_step, 1)
                        elif step == 2:
                            tt(xc2, x2, bc(mean2[:]), ALU.subtract).then_inc(ln2_step, 1)
                        elif step == 3:
                            tt(hn, xc2, xc2, ALU.mult).then_inc(ln2_step, 1)
                        elif step == 4:
                            nc.vector.tensor_reduce(sum2[:], hn, axis=AX_X, op=ALU.add).then_inc(ln2_step, 1)
                        elif step == 5:
                            ts(var2[:], sum2[:], 1.0 / D, EPS, ALU.mult, ALU.add).then_inc(var2_ready, 1)
                        elif step == 6:
                            dve.wait_ge(rstd2_ready, it)
                            stt(out=hn, in0=xc2, scalar=0.0, in1=bc(rstd2[:]), op0=ALU.max,
                                op1=ALU.mult).then_inc(hn_ready, 1)
                    elif name in ("Q", "K"):
                        half, bank = stage[1], ring.bank(stage)
                        hi, lo, hi_ready = {"Q": (q_hi, q_lo, q_hi_ready), "K": (k_hi, k_lo, k_hi_ready)}[name]
                        cols = slice(half * HALF, (half + 1) * HALF)
                        dve.wait_ge(hi_ready, (it - 1) * 2 + (half + 1))
                        tt(lo[:, cols], work_ps[:, bank, :], hi[:, cols].bitcast(F32), ALU.subtract).then_inc(work_read[bank], 1)
                    elif name == "max":
                        n = stage[1]
                        if n >= 2:
                            dve.wait_ge(exp_ready, (it - 1) * NPART + (n - 1))
                        dve.wait_ge(*ring.written(("S", n)))
                        nc.vector.memset(wait_carrier[:, n:n + 1], 0.0)
                        bank = ring.bank(("S", n))
                        for hh in range(2):
                            last = nc.vector.tensor_tensor_reduce(
                                out=masked[:, n % 2, hh, :], in0=work_ps[:, bank, hh * T:(hh + 1) * T],
                                in1=mask[:, n // 2 % 2, :], scale=1.0, scalar=BIGGEST, op0=ALU.add, op1=ALU.min,
                                accum_out=neg_max[:, 2 * n + hh:2 * n + hh + 1])
                        last.then_inc(work_read[bank], 1)
                    elif name == "out":
                        r, g = stage[1], it - 1
                        n = (r + 1) * (NPART // 2) - 1
                        dve.wait_ge(exp_ready, g * NPART + (n + 1))
                        nc.vector.reciprocal(prob_rec[:], prob_sum[:, r * NPART:(r + 1) * NPART]).then_inc(rec_ready, 1)
                        dve.wait_ge(rec_ready, g * 2 + (r + 1))
                        dve.wait_ge(av_done, g * NPART + (n + 1))
                        if r == 0:
                            dve.wait_ge(stored, it * 16)
                        ys = y[:, 4 * r:4 * r + 4, :]
                        tt(ys.rearrange("p t (h d) -> p (t h) d", d=HD), av_ps[:].rearrange("p (a d) -> p a d", d=HD),
                           prob_rec[:].unsqueeze(2).to_broadcast([P, NPART, HD]), ALU.mult).then_inc(av_read, 1)
                        dve.wait_ge(av_read, g * 2 + (r + 1))
                        tt(ys, ys, x2[:, 4 * r:4 * r + 4, :], ALU.add).then_inc(y_ready, 1)

            run(dve, iteration)


INPUTS = ["x", "adj", "L0_gnn_Wg0", "L0_gnn_bg0", "L0_gnn_Wg1", "L0_gnn_bg1", "L0_gnn_Wih", "L0_gnn_Whh",
          "L0_gnn_bih", "L0_gnn_bhh", "L1_gnn_W"]


def kernel(**inputs):
    import numpy as np
    import concourse.bacc as bacc
    from concourse.bass_utils import run_bass_kernel_spmd

    nc = bacc.Bacc("TRN2", target_bir_lowering=False, num_devices=1)
    arrays, args = {}, []
    for name in INPUTS:
        a = np.ascontiguousarray(inputs[name])
        arrays[f"in_{name}"] = a
        args.append(nc.dram_tensor(f"in_{name}", a.shape, mybir.dt.from_np(a.dtype), kind="ExternalInput").ap())
    args.append(nc.dram_tensor("out", (B, T, D), F32, kind="ExternalOutput").ap())
    graph_block(nc, *args)
    r = run_bass_kernel_spmd(nc, [arrays], core_ids=[0])
    return r.results[0]["out"]
```

```python
from contextlib import ExitStack

import concourse.bass as bass
from concourse import mybir

P = 128
B, T, D = 32, 256, 128
GB = 4
NG = B // GB
NT = GB * T // P
COLS = GB * T
HALF = COLS // 2
BANK = 512
HEADS, HD = 4, 32
MAX_SKIP = 4
EPS = 1e-5
MASKED = 1e30
BIGGEST = 3e38

F32 = mybir.dt.float32
F32R = mybir.dt.float32r
ALU = mybir.AluOpType
ACT = mybir.ActivationFunctionType
AX_X = mybir.AxisListType.X

GATE_I, GATE_G, GATE_F, GATE_O = range(4)
REF_BLOCK = {GATE_I: 0, GATE_F: 1, GATE_G: 2, GATE_O: 3}

STEPS = [(1, 0, HALF), (1, 0, HALF)]
STEPS += [(p, k, GB * (T // p)) for p in range(2, MAX_SKIP + 1) for k in range(p)]
NS = len(STEPS)


def gates_of(s):
    return (GATE_I, GATE_G, GATE_O) if STEPS[s][1] == 0 else (GATE_I, GATE_G, GATE_F, GATE_O)


GATE_NO = {}
for _s in range(NS):
    for _gate in gates_of(_s):
        GATE_NO[_s, _gate] = len(GATE_NO) + 1
GATES_PER_GROUP = len(GATE_NO)
UV_NO = {s: 2 * n for n, s in enumerate(s for s in range(NS) if STEPS[s][1])}
UV_PER_GROUP = 2 * len(UV_NO)

NPART = 2 * NT
STACK_DMAS = 2 * 4
SET_UP_DVE = 19

FIRST = {
    "tensor": [
        ("x", 0, 0), ("x", 0, 1), ("x", 1, 0), ("x", 1, 1), ("G1", 0), ("G1", 1), ("x", 2, 0), ("G2", 0),
        ("x", 3, 0), ("G2", 1), ("x", 2, 1), ("x", 3, 1), ("G3", 0), ("h", 3, 0), ("h", 3, 1), ("G3", 1),
        ("x", 4, 0), ("x", 4, 1), ("x", 5, 0), ("x", 5, 1), ("h", 5, 0), ("h", 5, 1), ("x", 6, 0),
        ("x", 6, 1), ("G4", 0), ("h", 6, 0), ("h", 6, 1), ("x", 7, 0), ("x", 7, 1), ("x", 8, 0),
        ("x", 8, 1), ("h", 8, 0), ("h", 8, 1), ("x", 9, 0), ("x", 9, 1), ("h", 9, 0), ("h", 9, 1),
        ("x", 10, 0), ("G4", 1), ("x", 10, 1), ("h", 10, 0), ("h", 10, 1),
    ],
    "scalar": [
        ("gates", 0, 0), ("gates", 0, 1), ("gates", 1, 0), ("tanh", 0), ("tanh", 1), ("gates", 1, 1),
        ("G1", 0), ("G1", 1), ("gates", 2, 0), ("gates", 2, 1), ("G2", 0), ("tanh", 2), ("gates", 3, 0),
        ("gates", 3, 1), ("G2", 1), ("tanh", 3), ("gates", 4, 0), ("gates", 4, 1), ("tanh", 4),
        ("gates", 5, 0), ("gates", 5, 1), ("tanh", 5), ("gates", 6, 0), ("gates", 6, 1), ("G4", 0),
        ("tanh", 6), ("gates", 7, 0), ("gates", 7, 1), ("tanh", 7), ("gates", 8, 0), ("gates", 8, 1),
        ("tanh", 8), ("gates", 9, 0), ("gates", 9, 1), ("tanh", 9), ("gates", 10, 0), ("gates", 10, 1),
        ("tanh", 10), ("G4", 1),
    ],
    "vector": [
        ("c", 0), ("L1", 0), ("c", 1), ("h", 0), ("h", 1), ("c", 2), ("G2", 0), ("L1", 1), ("h", 2),
        ("G2", 1), ("G3", 0), ("u", 3), ("c", 3), ("h", 3), ("c", 4), ("G3", 1), ("h", 4), ("u", 5),
        ("c", 5), ("h", 5), ("L1", 2), ("u", 6), ("L1", 3), ("c", 6), ("h", 6), ("G4", 0), ("L1", 4),
        ("c", 7), ("h", 7), ("u", 8), ("c", 8), ("h", 8), ("u", 9), ("c", 9), ("h", 9), ("u", 10),
        ("c", 10), ("h", 10), ("G4", 1),
    ],
}
MIDDLE = {
    "tensor": [
        ("x", 0, 0), ("T1", 0), ("x", 0, 1), ("T1", 1), ("x", 1, 0), ("G1", 0), ("x", 1, 1), ("G1", 1),
        ("x", 2, 0), ("G2", 0), ("x", 2, 1), ("x", 3, 0), ("G2", 1), ("x", 3, 1), ("G3", 0), ("T2", 0),
        ("G3", 1), ("Q", 0), ("h", 3, 0), ("h", 3, 1), ("T2", 1), ("G4", 0), ("K", 0), ("G4", 1), ("Q", 1),
        ("x", 4, 0), ("x", 4, 1), ("V", 0), ("V", 1), ("x", 5, 0), ("h", 5, 0), ("S", 0), ("x", 5, 1),
        ("S", 1), ("h", 5, 1), ("x", 6, 0), ("PT", 0), ("S", 2), ("K", 1), ("x", 6, 1), ("S", 3), ("PT", 1),
        ("h", 6, 0), ("h", 6, 1), ("S", 4), ("AV", 0), ("PT", 2), ("S", 5), ("S", 6), ("AV", 1), ("PT", 3),
        ("S", 7), ("AV", 2), ("PT", 4), ("AV", 3), ("PT", 5), ("AV", 4), ("S", 8), ("x", 7, 0), ("x", 7, 1),
        ("S", 9), ("S", 10), ("PT", 6), ("x", 8, 0), ("AV", 5), ("PT", 7), ("AV", 6), ("h", 8, 0),
        ("AV", 7), ("S", 11), ("x", 8, 1), ("h", 8, 1), ("PT", 8), ("x", 9, 0), ("x", 9, 1), ("PT", 9),
        ("AV", 8), ("S", 12), ("S", 13), ("PT", 10), ("h", 9, 0), ("h", 9, 1), ("PT", 11), ("AV", 9),
        ("x", 10, 0), ("AV", 10), ("S", 14), ("PT", 12), ("S", 15), ("AV", 11), ("PT", 13), ("x", 10, 1),
        ("h", 10, 0), ("AV", 12), ("PT", 14), ("h", 10, 1), ("AV", 13), ("PT", 15), ("AV", 14), ("AV", 15),
    ],
    "scalar": [
        ("gates", 0, 0), ("gates", 0, 1), ("gates", 1, 0), ("tanh", 0), ("tanh", 1), ("G1", 0),
        ("gates", 1, 1), ("gates", 2, 0), ("G1", 1), ("gates", 2, 1), ("G2", 0), ("tanh", 2), ("G2", 1),
        ("T2", 0), ("Q", 0), ("gates", 3, 0), ("gates", 3, 1), ("T2", 1), ("G4", 0), ("K", 0), ("tanh", 3),
        ("G4", 1), ("Q", 1), ("gates", 4, 0), ("gates", 4, 1), ("tanh", 4), ("V", 0), ("V", 1),
        ("gates", 5, 0), ("exp", 0), ("gates", 5, 1), ("exp", 1), ("tanh", 5), ("PT", 0), ("K", 1),
        ("exp", 2), ("PT", 1), ("gates", 6, 0), ("exp", 3), ("gates", 6, 1), ("PT", 2), ("exp", 4),
        ("PT", 3), ("exp", 5), ("PT", 4), ("tanh", 6), ("exp", 6), ("PT", 5), ("exp", 7), ("gates", 7, 0),
        ("gates", 7, 1), ("PT", 6), ("tanh", 7), ("exp", 8), ("PT", 7), ("gates", 8, 0), ("exp", 9),
        ("gates", 8, 1), ("PT", 8), ("exp", 10), ("tanh", 8), ("PT", 9), ("exp", 11), ("PT", 10),
        ("gates", 9, 0), ("gates", 9, 1), ("exp", 12), ("PT", 11), ("tanh", 9), ("exp", 13), ("PT", 12),
        ("exp", 14), ("PT", 13), ("gates", 10, 0), ("exp", 15), ("PT", 14), ("gates", 10, 1), ("PT", 15),
        ("tanh", 10),
    ],
    "vector": [
        ("T1", 0), ("c", 0), ("T1", 1), ("L2", 0), ("c", 1), ("h", 0), ("L2", 1), ("h", 1), ("L2", 2),
        ("L2", 3), ("L2", 4), ("L2", 5), ("G2", 0), ("G2", 1), ("c", 2), ("L2", 6), ("G3", 0), ("h", 2),
        ("G3", 1), ("L1", 0), ("Q", 0), ("u", 3), ("L1", 1), ("c", 3), ("G4", 0), ("K", 0), ("h", 3),
        ("G4", 1), ("Q", 1), ("c", 4), ("h", 4), ("max", 0), ("u", 5), ("max", 1), ("c", 5), ("max", 2),
        ("h", 5), ("max", 3), ("K", 1), ("L1", 2), ("max", 4), ("u", 6), ("max", 5), ("c", 6), ("max", 6),
        ("max", 7), ("h", 6), ("max", 8), ("c", 7), ("h", 7), ("max", 9), ("out", 0), ("max", 10),
        ("L1", 3), ("u", 8), ("c", 8), ("max", 11), ("h", 8), ("max", 12), ("u", 9), ("c", 9), ("max", 13),
        ("h", 9), ("max", 14), ("L1", 4), ("max", 15), ("u", 10), ("c", 10), ("h", 10), ("out", 1),
    ],
}
LAST = {
    "tensor": [
        ("T1", 0), ("T1", 1), ("T2", 0), ("T2", 1), ("Q", 0), ("K", 0), ("Q", 1), ("V", 0), ("V", 1),
        ("S", 0), ("S", 1), ("S", 2), ("S", 3), ("PT", 0), ("K", 1), ("S", 4), ("PT", 1), ("AV", 0),
        ("S", 5), ("PT", 2), ("AV", 1), ("PT", 3), ("S", 6), ("AV", 2), ("PT", 4), ("S", 7), ("AV", 3),
        ("PT", 5), ("AV", 4), ("S", 8), ("PT", 6), ("AV", 5), ("S", 9), ("PT", 7), ("AV", 6), ("S", 10),
        ("AV", 7), ("S", 11), ("PT", 8), ("PT", 9), ("AV", 8), ("S", 12), ("S", 13), ("PT", 10), ("AV", 9),
        ("PT", 11), ("S", 14), ("AV", 10), ("PT", 12), ("AV", 11), ("S", 15), ("PT", 13), ("AV", 12),
        ("PT", 14), ("AV", 13), ("PT", 15), ("AV", 14), ("AV", 15),
    ],
    "scalar": [
        ("T2", 0), ("T2", 1), ("Q", 0), ("K", 0), ("V", 0), ("Q", 1), ("V", 1), ("exp", 0), ("exp", 1),
        ("PT", 0), ("exp", 2), ("K", 1), ("PT", 1), ("exp", 3), ("PT", 2), ("exp", 4), ("PT", 3),
        ("exp", 5), ("PT", 4), ("exp", 6), ("PT", 5), ("exp", 7), ("PT", 6), ("PT", 7), ("exp", 8),
        ("exp", 9), ("PT", 8), ("exp", 10), ("PT", 9), ("exp", 11), ("PT", 10), ("exp", 12), ("PT", 11),
        ("exp", 13), ("PT", 12), ("exp", 14), ("PT", 13), ("exp", 15), ("PT", 14), ("PT", 15),
    ],
    "vector": [
        ("T1", 0), ("T1", 1), ("L2", 0), ("L2", 1), ("L2", 2), ("L2", 3), ("L2", 4), ("L2", 5), ("L2", 6),
        ("Q", 0), ("K", 0), ("Q", 1), ("max", 0), ("max", 1), ("max", 2), ("max", 3), ("K", 1), ("max", 4),
        ("max", 5), ("max", 6), ("max", 7), ("max", 8), ("max", 9), ("max", 10), ("out", 0), ("max", 11),
        ("max", 12), ("max", 13), ("max", 14), ("max", 15), ("out", 1),
    ],
}


def part_of(stage):
    name = stage[0]
    if name in ("x", "h", "gates", "u", "c", "tanh"):
        return "lstm"
    if name == "L1":
        return "ln1"
    return "gcn" if name[0] == "G" else "attn"


def stages(engine, parts):
    orders = LAST if parts == ("attn",) else MIDDLE if "attn" in parts else FIRST
    return [stage for stage in orders[engine] if part_of(stage) in parts]


def ring_uses(parts):
    uses = {}
    for stage in stages("tensor", parts):
        if stage[0] in ("T1", "T2", "Q", "K", "V", "G1", "G2", "G3", "G4", "S"):
            uses[stage] = len(uses)
    return uses


ALL = ("ln1", "gcn", "lstm", "attn")
GCN_USES, ALL_USES = len(ring_uses(("gcn",))), len(ring_uses(ALL))
ATTN_USES = len(ring_uses(("lstm", "attn")))


def uses_before(it):
    if isinstance(it, int) and it <= 0:
        return GCN_USES * max(it + 1, 0)
    if isinstance(it, int) and it == NG:
        return 2 * GCN_USES + ALL_USES * (NG - 2) + ATTN_USES
    return it * ALL_USES + (2 * GCN_USES - ALL_USES)


class Ring:

    def __init__(self, it, parts, full, read):
        self.uses, self.before, self.full, self.read = ring_uses(parts), uses_before(it), full, read
        self.first = isinstance(it, int) and it < 0

    def bank(self, use):
        return self.uses[use] % 2

    def written(self, use):
        return self.full, self.before + (self.uses[use] + 1)

    def half_before(self):
        return self.before // 2 if isinstance(self.before, int) else self.half

    def was_read(self, use):
        n = self.uses[use]
        return self.read[n % 2], self.half_before() + (n // 2 + 1)

    def is_free(self, use):
        n = self.uses[use]
        if self.first and n < 2:
            return None
        return self.read[n % 2], self.half_before() + n // 2

    def before_was_read(self, bank):
        return self.read[bank], self.half_before()


def make_ring(it, parts, full, read):
    ring = Ring(it, parts, full, read)
    if not isinstance(it, int):
        ring.half = it * (ALL_USES // 2) + (GCN_USES - ALL_USES // 2)
    return ring


def graph_block(nc, x, adj, Wg0, bg0, Wg1, bg1, Wih, Whh, bih, bhh, Wqkv, out):
    with ExitStack() as ctx:
        def sb(name, shape, dt=F32):
            return ctx.enter_context(nc.sbuf_tensor(name, shape, dt))

        def sem(name):
            return ctx.enter_context(nc.semaphore(name))

        ident = sb("ident", [P, P])
        ones = sb("ones", [P, P])
        shared = sb("shared", [P, 4, NT, D])
        wih_nat = shared[:, 0:2].rearrange("p a t d -> p (a t) d")
        whh_nat = shared[:, 2:4].rearrange("p a t d -> p (a t) d")
        x2, xc2, hn, y = (shared[:, n] for n in range(4))
        wih_hi, wih_lo = (sb(n, [P, 4 * MAX_SKIP, P], F32R) for n in ("wih_hi", "wih_lo"))
        whh_hi, whh_lo = (sb(n, [P, 4 * (MAX_SKIP - 1), P], F32R) for n in ("whh_hi", "whh_lo"))
        bih_rows = sb("bih_rows", [4 * MAX_SKIP, P])
        bhh_rows = sb("bhh_rows", [4 * MAX_SKIP, P])
        gate_bias = sb("gate_bias", [P, MAX_SKIP, 4])
        wg0 = sb("wg0", [D, D])
        wg1 = sb("wg1", [D, D])
        bg0_col = sb("bg0_col", [D, 1])
        bg1_bc = sb("bg1_bc", [P, D])
        wqkv = sb("wqkv", [D, 3 * D])
        wqk = sb("wqk", [D, 2, D])
        adj_hi, adj_lo = (sb(n, [P, 2, T], F32R) for n in ("adj_hi", "adj_lo"))
        mask = sb("mask", [P, 2, T])
        bias0 = sb("bias0", [D, T])
        minus_half = sb("minus_half", [P, NT])

        mean1, sum1, var1, rstd1 = (sb(n, [P, NT]) for n in ("mean1", "sum1", "var1", "rstd1"))
        x_ln = sb("x_ln", [P, NT, D])
        h0_nat = sb("h0_nat", [P, NT, D])
        rows_hi, rows_lo = (sb(n, [P, NT, D], F32R) for n in ("rows_hi", "rows_lo"))
        z_t = sb("z_t", [P, COLS])
        h1_t = z_t
        y1_nat = sb("y1_nat", [P, NT, D])
        h2_hi, h2_lo = (sb(n, [P, COLS], F32R) for n in ("h2_hi", "h2_lo"))

        h_t = sb("h_t", [P, COLS])
        h_hi, h_lo = (sb(n, [P, COLS], F32R) for n in ("h_hi", "h_lo"))
        step_hi, step_lo = (sb(n, [P, BANK], F32R) for n in ("step_hi", "step_lo"))
        gate = sb("gate", [P, 2, 4, BANK])
        c2, tanh_c = (sb(n, [P, 2, BANK]) for n in ("c2", "tanh_c"))
        u, v, h_step = (sb(n, [P, BANK]) for n in ("u", "v", "h_step"))

        x_res = sb("x_res", [P, NT, D])
        mean2, sum2, var2, rstd2 = (sb(n, [P, NT]) for n in ("mean2", "sum2", "var2", "rstd2"))
        hn_t = sb("hn_t", [P, COLS])
        q_hi, q_lo, k_hi, k_lo = (sb(n, [P, COLS], F32R) for n in ("q_hi", "q_lo", "k_hi", "k_lo"))
        q_stack = sb("q_stack", [P, HEADS, COLS], F32R)
        k_stack = sb("k_stack", [P, HEADS, COLS], F32R)
        v_nat = sb("v_nat", [P, NT, D])
        masked = sb("masked", [P, 2, 2, T])
        adj_nat, adj_t = masked[:, 0], masked[:, 1]
        neg_max = sb("neg_max", [P, 2 * NPART])
        wait_carrier = sb("wait_carrier", [P, NPART])
        probs = sb("probs", [P, 2, 2, T])
        prob_sum = sb("prob_sum", [P, 2 * NPART])
        prob_rec = sb("prob_rec", [P, NPART])
        probs_t = sb("probs_t", [P, 2, BANK])

        gate_ps = ctx.enter_context(nc.psum_tensor("gate_ps", [P, 4, BANK], F32))
        work_ps = ctx.enter_context(nc.psum_tensor("work_ps", [P, 2, BANK], F32))
        pt_ps = ctx.enter_context(nc.psum_tensor("pt_ps", [P, BANK], F32))
        av_ps = ctx.enter_context(nc.psum_tensor("av_ps", [P, BANK], F32))

        adj_loaded, wih_loaded, whh_loaded = sem("adj_loaded"), sem("wih_loaded"), sem("whh_loaded")
        lstm_bias_loaded, small_loaded = sem("lstm_bias_loaded"), sem("small_loaded")
        x_ln_loaded, x_res_loaded = sem("x_ln_loaded"), sem("x_res_loaded")
        zeroed, ident_ready, ones_ready, set_up_t, set_up_act, set_up_dve = (
            sem(n) for n in ("zeroed", "ident_ready", "ones_ready", "set_up_t", "set_up_act", "set_up_dve"))
        work_full = sem("work_full")
        work_read = [sem("work_read0"), sem("work_read1")]
        ln1_step, mean1_ready, xc1_ready, sq1_ready, var1_ready, rstd1_ready, h0_ready = (
            sem(n) for n in ("ln1_step", "mean1_ready", "xc1_ready", "sq1_ready", "var1_ready",
                             "rstd1_ready", "h0_ready"))
        h0_hi_ready, h0_split, y1_hi_ready, y1_split = (
            sem(n) for n in ("h0_hi_ready", "h0_split", "y1_hi_ready", "y1_split"))
        ln2_step, var2_ready, rstd2_ready, hn_ready = (
            sem(n) for n in ("ln2_step", "var2_ready", "rstd2_ready", "hn_ready"))
        h1_ready = sem("h1_ready")
        gate_full, gate_ready, uv_ready, c_ready, tanh_c_ready, h_ready, h_hi_ready, h_lo_ready, h2_hi_ready = (
            sem(n) for n in ("gate_full", "gate_ready", "uv_ready", "c_ready", "tanh_c_ready", "h_ready",
                             "h_hi_ready", "h_lo_ready", "h2_hi_ready"))
        q_hi_ready, k_hi_ready = sem("q_hi_ready"), sem("k_hi_ready")
        stacked = [sem("stacked0"), sem("stacked1")]
        exp_ready, pt_full, pt_read, av_done, rec_ready, av_read, y_ready, stored = (
            sem(n) for n in ("exp_ready", "pt_full", "pt_read", "av_done", "rec_ready", "av_read",
                             "y_ready", "stored"))

        def ring_of(it, parts):
            return make_ring(it, parts, work_full, work_read)

        def window(t, s, order):
            p, k, _ = STEPS[s]
            if p == 1:
                return t[:].rearrange(f"f ({order}) -> f b t", b=GB)[:, s * GB // 2:(s + 1) * GB // 2, :]
            return t[:].rearrange(f"f ({order}) -> f t b", b=GB)[:, k:k + (T // p - 1) * p + 1:p, :]

        def as_window(ap, s):
            if STEPS[s][0] == 1:
                return ap.rearrange("f (b t) -> f b t", t=T)
            return ap.rearrange("f (w b) -> f w b", b=GB)

        def first_group(g):
            return isinstance(g, int) and g == 0

        def cell_slot(s):
            return 1 if s == 1 else 0

        def run(eng, iteration):
            iteration(-2, ("ln1",))
            iteration(-1, ("ln1", "gcn"))
            iteration(0, ("ln1", "gcn", "lstm"))
            with eng.Fori(1, NG - 2) as it:
                iteration(it, ALL)
            iteration(NG - 2, ("gcn", "lstm", "attn"))
            iteration(NG - 1, ("lstm", "attn"))
            iteration(NG, ("attn",))

        block = ctx.enter_context(nc.Block())

        @block.sync
        def _(sp):
            sp.dma_start(adj_nat, adj.rearrange("(t p) s -> p t s", p=P)).then_inc(adj_loaded, 16)
            x_tiles = x.rearrange("b (h p) d -> p (b h) d", p=P)
            sp.dma_start(x_ln[:], x_tiles[:, 0:NT, :]).then_inc(x_ln_loaded, 16)
            sp.dma_start(wih_nat, Wih.rearrange("l (g p) d -> p (l g) d", p=P)).then_inc(wih_loaded, 16)
            sp.dma_start(whh_nat, Whh.rearrange("l (g p) d -> p (l g) d", p=P)).then_inc(whh_loaded, 16)
            out_tiles = out.rearrange("b (h p) d -> p (b h) d", p=P)
            sp.sem_inc(stored, 16)

            def stack_heads(ring, half):
                cols = slice(half * HALF, (half + 1) * HALF)
                for use, hi, lo, stack, quadrants in (("Q", q_hi, q_lo, q_stack, (0, 0, 1, 1)),
                                                      ("K", k_hi, k_lo, k_stack, (0, 1, 0, 1))):
                    sp.wait_ge(*ring.was_read((use, half)))
                    for quadrant, part in enumerate(quadrants):
                        sp.dma_start(stack[quadrant * HD:(quadrant + 1) * HD, :, cols].bitcast(F32),
                                     (hi, lo)[part][:, cols].bitcast(F32)).then_inc(stacked[half], 16)

            def iteration(it, parts):
                if "ln1" in parts and not (isinstance(it, int) and it < -1):
                    sp.wait_ge(h0_ready, it + 2)
                    sp.dma_start(x_ln[:], x_tiles[:, bass.ds((it + 2) * NT, NT), :]).then_inc(x_ln_loaded, 16)
                if "attn" in parts:
                    stack_heads(ring_of(it, parts), 0)
                    stack_heads(ring_of(it, parts), 1)
                if "lstm" in parts:
                    sp.dma_start(x_res[:], x_tiles[:, bass.ds(it * NT, NT), :]).then_inc(x_res_loaded, 16)
                if "attn" in parts:
                    sp.wait_ge(y_ready, (it + 1) * 2)
                    sp.dma_start(out_tiles[:, bass.ds((it - 1) * NT, NT), :], y).then_inc(stored, 16)

            run(sp, iteration)
            sp.wait_ge(stored, 16 * (NG + 1))

        @block.gpsimd
        def _(pool):
            nc.gpsimd.memset(ident[:], 0.0).then_inc(zeroed, 1)
            nc.gpsimd.memset(ones[:], 1.0).then_inc(ones_ready, 1)
            nc.gpsimd.memset(minus_half[:], -0.5).then_inc(zeroed, 1)
            pool.wait_ge(zeroed, 2)
            nc.gpsimd.affine_select(out=ident[:], in_=ident[:], compare_op=ALU.not_equal, fill=1.0, base=0,
                                    pattern=[[-1, P]], channel_multiplier=1).then_inc(ident_ready, 1)

            def iteration(it, parts):
                ring = ring_of(it, parts)
                if "attn" in parts:
                    pool.wait_ge(var2_ready, it)
                    nc.gpsimd.tensor_tensor(rstd2[:], var2[:], minus_half[:], ALU.pow).then_inc(rstd2_ready, 1)
                if "gcn" in parts and not first_group(it + 1):
                    for half in range(2):
                        tiles = slice(4 * half, 4 * half + 4)
                        pool.wait_ge(*ring.was_read(("G3", half)))
                        nc.gpsimd.tensor_tensor(rows_hi[:, tiles, :], y1_nat[:, tiles, :],
                                                ones[:].unsqueeze(1).to_broadcast([P, 4, D]),
                                                ALU.mult).then_inc(y1_hi_ready, 1)
                        pool.wait_ge(y1_hi_ready, it * 2 + (half + 1))
                        nc.gpsimd.tensor_tensor(rows_lo[:, tiles, :], y1_nat[:, tiles, :],
                                                rows_hi[:, tiles, :].bitcast(F32), ALU.subtract).then_inc(y1_split, 1)
                if "ln1" in parts:
                    g = it + 2
                    pool.wait_ge(mean1_ready, g + 1)
                    nc.gpsimd.tensor_tensor(x_ln[:], x_ln[:], mean1[:].unsqueeze(2).to_broadcast([P, NT, D]),
                                            ALU.subtract).then_inc(xc1_ready, 1)
                    pool.wait_ge(xc1_ready, g + 1)
                    if first_group(it + 1):
                        pool.wait_ge(*ring.written(("G1", 1)))
                    nc.gpsimd.tensor_tensor(h0_nat[:], x_ln[:], x_ln[:], ALU.mult).then_inc(sq1_ready, 1)
                    pool.wait_ge(var1_ready, g + 1)
                    nc.gpsimd.tensor_tensor(rstd1[:], var1[:], minus_half[:], ALU.pow).then_inc(rstd1_ready, 1)
                    if first_group(g):
                        return
                    pool.wait_ge(h0_ready, g + 1)
                    if "gcn" in parts and not first_group(it + 1):
                        pool.wait_ge(*ring.written(("G4", 1)))
                    nc.gpsimd.tensor_tensor(rows_hi[:], h0_nat[:], ones[:].unsqueeze(1).to_broadcast([P, NT, D]),
                                            ALU.mult).then_inc(h0_hi_ready, 1)
                    pool.wait_ge(h0_hi_ready, it + 2)
                    nc.gpsimd.tensor_tensor(rows_lo[:], h0_nat[:], rows_hi[:].bitcast(F32),
                                            ALU.subtract).then_inc(h0_split, 1)

            run(pool, iteration)

        @block.tensor
        def _(pe):
            mm = nc.tensor.matmul

            pe.wait_ge(ident_ready, 1)
            pe.wait_ge(adj_loaded, 16)
            for st in range(2):
                for tt in range(2):
                    last = nc.tensor.transpose(av_ps[:, st * T + tt * P:st * T + (tt + 1) * P],
                                               adj_nat[:, tt, st * P:(st + 1) * P], ident[:])
            last.then_inc(set_up_t, 1)
            pe.wait_ge(wih_loaded, 16)
            for p in range(MAX_SKIP):
                for blk in range(4):
                    last = nc.tensor.transpose(gate_ps[:, p, blk * P:(blk + 1) * P], wih_nat[:, 4 * p + blk, :],
                                               ident[:])
                last.then_inc(set_up_t, 1)
            pe.wait_ge(whh_loaded, 16)
            for p in range(1, MAX_SKIP):
                dst = work_ps[:, p - 1, :] if p < 3 else pt_ps[:]
                for blk in range(4):
                    last = nc.tensor.transpose(dst[:, blk * P:(blk + 1) * P], whh_nat[:, 4 * p + blk, :], ident[:])
                last.then_inc(set_up_t, 1)
            pe.wait_ge(set_up_dve, 4)
            pe.wait_ge(ones_ready, 1)
            for st in range(2):
                mm(av_ps[:, 0:T], ones[:], adj_t[:, st, :], start=st == 0, stop=st == 1)
            nc.tensor.transpose(av_ps[:, T:T + 4 * MAX_SKIP], bih_rows[:],
                                ident[0:4 * MAX_SKIP, 0:4 * MAX_SKIP]).then_inc(set_up_t, 1)
            pe.wait_ge(set_up_act, 7)
            pe.wait_ge(set_up_dve, SET_UP_DVE)

            def iteration(it, parts):
                ring = ring_of(it, parts)

                def claim(use):
                    free = ring.is_free(use)
                    if free is not None:
                        pe.wait_ge(*free)
                    return work_ps[:, ring.bank(use), :]

                def free_gate(s, gate_):
                    for back in range(s - 1, -1, -1):
                        if gate_ in gates_of(back):
                            pe.wait_ge(gate_ready, it * GATES_PER_GROUP + GATE_NO[back, gate_])
                            return
                    if isinstance(it, int) and it == 0:
                        return
                    pe.wait_ge(gate_ready, it * GATES_PER_GROUP + (GATE_NO[NS - 1, gate_] - GATES_PER_GROUP))

                for stage in stages("tensor", parts):
                    name = stage[0]
                    if name == "x":
                        s, part = stage[1:]
                        p, k, n = STEPS[s]
                        if p == 1:
                            pe.wait_ge(*ring.before_was_read(s))
                            x_hi, x_lo = (t[:, s * HALF:(s + 1) * HALF] for t in (h2_hi, h2_lo))
                        else:
                            if k == 0:
                                pe.wait_ge(h_hi_ready, it * NS + s)
                            x_hi, x_lo = window(h_hi, s, "t b"), window(h_lo, s, "t b")
                        which = gates_of(s)[2 * part:2 * part + 2]
                        for j in which:
                            free_gate(s, j)
                            blk, dst = 4 * (p - 1) + REF_BLOCK[j], gate_ps[:, j, 0:n]
                            mm(dst, wih_hi[:, blk, :], x_hi, start=True, stop=False)
                            mm(dst, wih_lo[:, blk, :], x_hi, start=False, stop=False)
                        if p > 1 and k == 0:
                            pe.wait_ge(h_lo_ready, it * NS + s)
                        for j in which:
                            blk, dst = 4 * (p - 1) + REF_BLOCK[j], gate_ps[:, j, 0:n]
                            last = mm(dst, wih_hi[:, blk, :], x_lo, start=False, stop=k == 0)
                            if k == 0:
                                last.then_inc(gate_full, 1)
                    elif name == "h":
                        s, part = stage[1:]
                        p, k, n = STEPS[s]
                        which = gates_of(s)[2 * part:2 * part + 2]
                        pe.wait_ge(h_hi_ready, it * NS + s)
                        for j in which:
                            blk, dst = 4 * (p - 2) + REF_BLOCK[j], gate_ps[:, j, 0:n]
                            mm(dst, whh_hi[:, blk, :], step_hi[:, 0:n], start=False, stop=False)
                            mm(dst, whh_lo[:, blk, :], step_hi[:, 0:n], start=False, stop=False)
                        pe.wait_ge(h_lo_ready, it * NS + s)
                        for j in which:
                            blk, dst = 4 * (p - 2) + REF_BLOCK[j], gate_ps[:, j, 0:n]
                            mm(dst, whh_hi[:, blk, :], step_lo[:, 0:n], start=False, stop=True).then_inc(gate_full, 1)
                    elif name in ("T1", "T2"):
                        half = stage[1]
                        if name == "T1":
                            pe.wait_ge(h_ready, it * NS)
                        else:
                            pe.wait_ge(hn_ready, it)
                        dst = claim(stage)
                        for t in range(4 * half, 4 * half + 4):
                            src = h_t[:, t * P:(t + 1) * P] if name == "T1" else hn[:, t, :]
                            last = nc.tensor.transpose(dst[:, t % 4 * P:(t % 4 + 1) * P], src, ident[:])
                        last.then_inc(work_full, 1)
                    elif name in ("Q", "K"):
                        half = stage[1]
                        pe.wait_ge(*ring.was_read(("T2", half)))
                        mm(claim(stage), wqk[:, "QK".index(name), :], hn_t[:, half * HALF:(half + 1) * HALF],
                           start=True, stop=True).then_inc(work_full, 1)
                    elif name == "V":
                        half = stage[1]
                        pe.wait_ge(*ring.was_read(("T2", half)))
                        dst = claim(stage)
                        for t in range(4):
                            last = mm(dst[:, t * D:(t + 1) * D], hn_t[:, (4 * half + t) * P:(4 * half + t + 1) * P],
                                      wqkv[:, 2 * D:3 * D], start=True, stop=True)
                        last.then_inc(work_full, 1)
                    elif name == "S":
                        n = stage[1]
                        dst = claim(stage)
                        if n % (NPART // 2) == 0:
                            pe.wait_ge(stacked[n // (NPART // 2)], it * STACK_DMAS * 16)
                        for hh in range(2):
                            head = 2 * (n % 2) + hh
                            last = mm(dst[:, hh * T:(hh + 1) * T], q_stack[:, head, n // 2 * P:(n // 2 + 1) * P],
                                      k_stack[:, head, n // 4 * T:(n // 4 + 1) * T], start=True, stop=True)
                        last.then_inc(work_full, 1)
                    elif name == "PT":
                        n = stage[1]
                        pe.wait_ge(exp_ready, (it - 1) * NPART + (n + 1))
                        if n:
                            pe.wait_ge(pt_read, (it - 1) * NPART + n)
                        for hk in range(4):
                            last = nc.tensor.transpose(pt_ps[:, hk * P:(hk + 1) * P],
                                                       probs[:, n % 2, hk // 2, (hk % 2) * P:(hk % 2 + 1) * P], ident[:])
                        last.then_inc(pt_full, 1)
                    elif name == "AV":
                        n = stage[1]
                        pe.wait_ge(pt_read, (it - 1) * NPART + (n + 1))
                        if n == 0:
                            pe.wait_ge(*ring.was_read(("V", 1)))
                        if n == NPART // 2:
                            pe.wait_ge(av_read, (it - 1) * 2 + 1)
                        for hh in range(2):
                            head, col = 2 * (n % 2) + hh, (n % (NPART // 2)) * 2 * HD + hh * HD
                            for kt in range(2):
                                last = mm(av_ps[:, col:col + HD],
                                          probs_t[:, n % 2, (2 * hh + kt) * P:(2 * hh + kt + 1) * P],
                                          v_nat[:, n // 4 * 2 + kt, head * HD:(head + 1) * HD],
                                          start=kt == 0, stop=kt == 1)
                        last.then_inc(av_done, 1)
                    elif name in ("G1", "G4"):
                        half = stage[1]
                        if first_group(it + 1):
                            if name == "G1":
                                src = h0_nat
                                pe.wait_ge(h0_ready, 1)
                            else:
                                src = y1_nat
                                pe.wait_ge(*ring.was_read(("G3", half)))
                            dst = claim(stage)
                            for b in range(2):
                                for st in range(2):
                                    last = mm(dst[:, b * T:(b + 1) * T], src[:, 4 * half + 2 * b + st, :],
                                              adj_t[:, st, :], start=st == 0, stop=st == 1)
                            last.then_inc(work_full, 1)
                            continue
                        if name == "G1":
                            pe.wait_ge(h0_split, it + 1)
                        else:
                            pe.wait_ge(y1_split, it * 2 + (half + 1))
                        dst = claim(stage)
                        for b in range(2):
                            for st in range(2):
                                cols, tile = dst[:, b * T:(b + 1) * T], 4 * half + 2 * b + st
                                mm(cols, rows_hi[:, tile, :], adj_hi[:, st, :], start=st == 0, stop=False)
                                mm(cols, rows_hi[:, tile, :], adj_lo[:, st, :], start=False, stop=False)
                                last = mm(cols, rows_lo[:, tile, :], adj_hi[:, st, :], start=False, stop=st == 1)
                        last.then_inc(work_full, 1)
                    elif name == "G2":
                        half = stage[1]
                        pe.wait_ge(*ring.was_read(("G1", half)))
                        mm(claim(stage), wg0[:], z_t[:, half * HALF:(half + 1) * HALF],
                           start=True, stop=True).then_inc(work_full, 1)
                    elif name == "G3":
                        half = stage[1]
                        pe.wait_ge(h1_ready, (it + 1) * 2 + (half + 1))
                        dst = claim(stage)
                        for t in range(4):
                            last = mm(dst[:, t * D:(t + 1) * D], h1_t[:, (4 * half + t) * P:(4 * half + t + 1) * P],
                                      wg1[:], start=True, stop=True)
                        last.then_inc(work_full, 1)

            run(pe, iteration)

        @block.scalar
        def _(act):
            act.dma_start(bih_rows[:], bih.rearrange("l (g p) -> (l g) p", p=P)).then_inc(lstm_bias_loaded, 16)
            act.dma_start(bhh_rows[:], bhh.rearrange("l (g p) -> (l g) p", p=P)).then_inc(lstm_bias_loaded, 16)
            act.dma_start(wg0[:], Wg0).then_inc(small_loaded, 16)
            act.dma_start(wg1[:], Wg1).then_inc(small_loaded, 16)
            act.dma_start(wqkv[:], Wqkv).then_inc(small_loaded, 16)
            act.dma_start(bg0_col[:], bg0.rearrange("(p a) -> p a", a=1)).then_inc(small_loaded, 16)
            act.dma_start(bg1_bc[:], bg1.partition_broadcast(P)).then_inc(small_loaded, 16)
            for p in range(MAX_SKIP):
                act.wait_ge(set_up_t, 2 + p)
                nc.scalar.activation(wih_hi[:, 4 * p:4 * p + 4, :].rearrange("f g r -> f (g r)"), gate_ps[:, p, :], ACT.Copy,
                                     scale=0.5 if p else 1.0).then_inc(set_up_act, 1)
            for p in range(1, MAX_SKIP):
                act.wait_ge(set_up_t, 5 + p)
                src = work_ps[:, p - 1, :] if p < 3 else pt_ps[:]
                nc.scalar.activation(whh_hi[:, 4 * p - 4:4 * p, :].rearrange("f g r -> f (g r)"), src, ACT.Copy,
                                     scale=0.5).then_inc(set_up_act, 1)
            act.wait_ge(set_up_dve, SET_UP_DVE)

            def iteration(it, parts):
                ring = ring_of(it, parts)

                for stage in stages("scalar", parts):
                    name = stage[0]
                    if name == "gates":
                        s, part = stage[1:]
                        p, k, n = STEPS[s]
                        if stage == ("gates", 0, 0) and not (isinstance(it, int) and it == 0):
                            act.wait_ge(h_ready, it * NS)
                        for j in gates_of(s)[2 * part:2 * part + 2]:
                            act.wait_ge(gate_full, it * GATES_PER_GROUP + GATE_NO[s, j])
                            nc.scalar.activation(gate[:, s % 2, j, 0:n], gate_ps[:, j, 0:n], ACT.Tanh,
                                                 bias=gate_bias[:, p - 1, REF_BLOCK[j]:REF_BLOCK[j] + 1],
                                                 scale=1.0 if j == GATE_G else 0.5).then_inc(gate_ready, 1)
                    elif name == "tanh":
                        s = stage[1]
                        n = STEPS[s][2]
                        act.wait_ge(c_ready, it * NS + (s + 1))
                        nc.scalar.activation(tanh_c[:, cell_slot(s), 0:n], c2[:, cell_slot(s), 0:n], ACT.Tanh,
                                             scale=0.5).then_inc(tanh_c_ready, 1)
                    elif name == "G2":
                        act.wait_ge(*ring.was_read(stage))
                        half = stage[1]
                        cols = h1_t[:, half * HALF:(half + 1) * HALF]
                        nc.scalar.activation(cols, cols, ACT.Relu).then_inc(h1_ready, 1)
                    elif name in ("Q", "K", "G4"):
                        act.wait_ge(*ring.written(stage))
                        half = stage[1]
                        dst, ready, func = {"Q": (q_hi, q_hi_ready, ACT.Copy), "K": (k_hi, k_hi_ready, ACT.Copy),
                                            "G4": (h2_hi, h2_hi_ready, ACT.Relu)}[name]
                        nc.scalar.activation(dst[:, half * HALF:(half + 1) * HALF], work_ps[:, ring.bank(stage), :],
                                             func).then_inc(ready, 1)
                    elif name in ("T2", "V", "G1"):
                        act.wait_ge(*ring.written(stage))
                        half = stage[1]
                        dst = v_nat[:].rearrange("p t d -> p (t d)") if name == "V" else (hn_t if name == "T2" else z_t)[:]
                        nc.scalar.activation(dst[:, half * HALF:(half + 1) * HALF], work_ps[:, ring.bank(stage), :],
                                             ACT.Copy).then_inc(work_read[ring.bank(stage)], 1)
                    elif name == "exp":
                        n = stage[1]
                        act.wait_ge(*ring.was_read(("S", n)))
                        if n >= 2:
                            act.wait_ge(pt_full, (it - 1) * NPART + (n - 1))
                        for hh in range(2):
                            last = nc.scalar.activation(probs[:, n % 2, hh, :], masked[:, n % 2, hh, :], ACT.Exp,
                                                        scale=-1.0, bias=neg_max[:, 2 * n + hh:2 * n + hh + 1],
                                                        accum_out=prob_sum[:, 2 * n + hh:2 * n + hh + 1])
                        last.then_inc(exp_ready, 1)
                    elif name == "PT":
                        n = stage[1]
                        act.wait_ge(pt_full, (it - 1) * NPART + (n + 1))
                        if n >= 2:
                            act.wait_ge(av_done, (it - 1) * NPART + (n - 1))
                        nc.scalar.activation(probs_t[:, n % 2, :], pt_ps[:], ACT.Copy).then_inc(pt_read, 1)

            run(act, iteration)

        @block.vector
        def _(dve):
            tt, stt, ts = nc.vector.tensor_tensor, nc.vector.scalar_tensor_tensor, nc.vector.tensor_scalar

            def row_sums(g):
                dve.wait_ge(x_ln_loaded, (g + 1) * 16)
                nc.vector.tensor_reduce(sum1[:], x_ln[:], axis=AX_X, op=ALU.add).then_inc(ln1_step, 1)

            def means(g):
                dve.wait_ge(ln1_step, g * 2 + 1)
                ts(mean1[:], sum1[:], 1.0 / D, None, ALU.mult).then_inc(mean1_ready, 1)

            dve.wait_ge(set_up_t, 1)
            nc.vector.tensor_copy(adj_t.rearrange("p a t -> p (a t)"), av_ps[:]).then_inc(set_up_dve, 1)
            nc.vector.tensor_copy(adj_hi[:].rearrange("p a t -> p (a t)"), av_ps[:]).then_inc(set_up_dve, 1)
            dve.wait_ge(set_up_dve, 2)
            tt(adj_lo[:], adj_t, adj_hi[:].bitcast(F32), ALU.subtract).then_inc(set_up_dve, 1)
            dve.wait_ge(lstm_bias_loaded, 32)
            tt(bih_rows[:], bih_rows[:], bhh_rows[:], ALU.add).then_inc(set_up_dve, 1)
            ts(mask[:], adj_nat, 0.0, MASKED, ALU.is_equal, ALU.mult).then_inc(set_up_dve, 1)
            row_sums(0)
            means(0)
            for p in range(MAX_SKIP):
                dve.wait_ge(set_up_act, 1 + p)
                stt(out=wih_lo[:, 4 * p:4 * p + 4, :].rearrange("f g r -> f (g r)"), in0=gate_ps[:, p, :],
                    scalar=0.5 if p else 1.0, in1=wih_hi[:, 4 * p:4 * p + 4, :].rearrange("f g r -> f (g r)").bitcast(F32),
                    op0=ALU.mult, op1=ALU.subtract).then_inc(set_up_dve, 1)
            for p in range(1, MAX_SKIP):
                dve.wait_ge(set_up_act, 4 + p)
                src = work_ps[:, p - 1, :] if p < 3 else pt_ps[:]
                stt(out=whh_lo[:, 4 * p - 4:4 * p, :].rearrange("f g r -> f (g r)"), in0=src, scalar=0.5,
                    in1=whh_hi[:, 4 * p - 4:4 * p, :].rearrange("f g r -> f (g r)").bitcast(F32),
                    op0=ALU.mult, op1=ALU.subtract).then_inc(set_up_dve, 1)
            dve.wait_ge(set_up_t, 9)
            dve.wait_ge(small_loaded, 80)
            ts(bias0[:], av_ps[:, 0:T], bg0_col[:, 0:1], None, ALU.mult).then_inc(set_up_dve, 1)
            bias_cols = av_ps[:, T:T + 4 * MAX_SKIP].rearrange("p (l g) -> p l g", g=4)
            for blk in range(4):
                ts(gate_bias[:, :, blk:blk + 1], bias_cols[:, :, blk:blk + 1], 1.0 if blk == REF_BLOCK[GATE_G] else 0.5,
                   None, ALU.mult).then_inc(set_up_dve, 1)
            for col, scale in enumerate((-float(HD) ** -0.5, 1.0)):
                ts(wqk[:, col, :].rearrange("f (d h) -> f d h", h=HEADS),
                   wqkv[:, col * D:(col + 1) * D].rearrange("f (h d) -> f d h", h=HEADS), scale, None,
                   ALU.mult).then_inc(set_up_dve, 1)

            dve.sem_inc(y_ready, 2)

            def iteration(it, parts):
                ring = ring_of(it, parts)

                def bc(stat):
                    return stat.unsqueeze(2).to_broadcast([P, NT, D])

                for stage in stages("vector", parts):
                    name = stage[0]
                    if name == "L1":
                        g, step = it + 2, stage[1]
                        if step < 2:
                            if not (isinstance(it, int) and it == -2):
                                (row_sums, means)[step](g)
                        elif step == 2:
                            dve.wait_ge(sq1_ready, g + 1)
                            nc.vector.tensor_reduce(sum1[:], h0_nat[:], axis=AX_X, op=ALU.add).then_inc(ln1_step, 1)
                        elif step == 3:
                            dve.wait_ge(ln1_step, g * 2 + 2)
                            ts(var1[:], sum1[:], 1.0 / D, EPS, ALU.mult, ALU.add).then_inc(var1_ready, 1)
                        else:
                            dve.wait_ge(rstd1_ready, g + 1)
                            stt(out=h0_nat[:], in0=x_ln[:], scalar=0.0, in1=bc(rstd1[:]), op0=ALU.max,
                                op1=ALU.mult).then_inc(h0_ready, 1)
                    elif name == "G2":
                        dve.wait_ge(*ring.written(stage))
                        half, bank = stage[1], ring.bank(stage)
                        tt(h1_t[:, half * HALF:(half + 1) * HALF].rearrange("f (b t) -> f b t", b=2),
                           work_ps[:, bank, :].rearrange("f (b t) -> f b t", b=2),
                           bias0[:].unsqueeze(1).to_broadcast([D, 2, T]), ALU.add).then_inc(work_read[bank], 1)
                    elif name == "G3":
                        dve.wait_ge(*ring.written(stage))
                        half, bank = stage[1], ring.bank(stage)
                        tt(y1_nat[:, 4 * half:4 * half + 4, :], work_ps[:, bank, :].rearrange("p (t d) -> p t d", d=D),
                           bg1_bc[:].unsqueeze(1).to_broadcast([P, 4, D]), ALU.add).then_inc(work_read[bank], 1)
                    elif name == "G4":
                        half, bank = stage[1], ring.bank(stage)
                        cols = slice(half * HALF, (half + 1) * HALF)
                        dve.wait_ge(h2_hi_ready, (it + 1) * 2 + (half + 1))
                        stt(out=h2_lo[:, cols], in0=work_ps[:, bank, :], scalar=0.0, in1=h2_hi[:, cols].bitcast(F32),
                            op0=ALU.max, op1=ALU.subtract).then_inc(work_read[bank], 1)
                    elif name == "u":
                        s = stage[1]
                        n = STEPS[s][2]
                        dve.wait_ge(gate_ready, it * GATES_PER_GROUP + GATE_NO[s, GATE_G])
                        stt(out=u[:, 0:n], in0=gate[:, s % 2, GATE_I, 0:n], scalar=1.0, in1=gate[:, s % 2, GATE_G, 0:n],
                            op0=ALU.add, op1=ALU.mult).then_inc(uv_ready, 1)
                    elif name == "c":
                        s = stage[1]
                        p, k, n = STEPS[s]
                        c_now = c2[:, cell_slot(s), 0:n]
                        if k == 0:
                            dve.wait_ge(gate_ready, it * GATES_PER_GROUP + GATE_NO[s, GATE_G])
                            stt(out=c_now, in0=gate[:, s % 2, GATE_I, 0:n], scalar=1.0, in1=gate[:, s % 2, GATE_G, 0:n],
                                op0=ALU.add, op1=ALU.mult).then_inc(c_ready, 1)
                        else:
                            dve.wait_ge(gate_ready, it * GATES_PER_GROUP + GATE_NO[s, GATE_F])
                            stt(out=v[:, 0:n], in0=gate[:, s % 2, GATE_F, 0:n], scalar=1.0, in1=c_now,
                                op0=ALU.add, op1=ALU.mult).then_inc(uv_ready, 1)
                            dve.wait_ge(uv_ready, it * UV_PER_GROUP + (UV_NO[s] + 2))
                            stt(out=c_now, in0=v[:, 0:n], scalar=0.5, in1=u[:, 0:n],
                                op0=ALU.mult, op1=ALU.add).then_inc(c_ready, 1)
                    elif name == "h":
                        s = stage[1]
                        p, k, n = STEPS[s]
                        dve.wait_ge(tanh_c_ready, it * NS + (s + 1))
                        dve.wait_ge(gate_ready, it * GATES_PER_GROUP + GATE_NO[s, GATE_O])
                        if s == 0 and "attn" in parts:
                            dve.wait_ge(*ring.written(("T1", 1)))
                        if k == p - 1:
                            whole, hi, lo = window(h_t, s, "b t"), window(h_hi, s, "t b"), window(h_lo, s, "t b")
                        else:
                            whole, hi, lo = (as_window(t[:, 0:n], s) for t in (h_step, step_hi, step_lo))
                        stt(out=whole, in0=as_window(gate[:, s % 2, GATE_O, 0:n], s), scalar=1.0,
                            in1=as_window(tanh_c[:, cell_slot(s), 0:n], s), op0=ALU.add, op1=ALU.mult).then_inc(h_ready, 1)
                        dve.wait_ge(h_ready, it * NS + (s + 1))
                        nc.vector.tensor_copy(hi, whole).then_inc(h_hi_ready, 1)
                        dve.wait_ge(h_hi_ready, it * NS + (s + 1))
                        tt(lo, whole, hi.bitcast(F32), ALU.subtract).then_inc(h_lo_ready, 1)
                    elif name == "T1":
                        half, bank = stage[1], ring.bank(stage)
                        dve.wait_ge(y_ready, it * 2)
                        dve.wait_ge(x_res_loaded, it * 16)
                        dve.wait_ge(*ring.written(stage))
                        stt(out=x2[:, 4 * half:4 * half + 4, :].rearrange("p t d -> p (t d)"),
                            in0=work_ps[:, bank, :], scalar=0.5,
                            in1=x_res[:, 4 * half:4 * half + 4, :].rearrange("p t d -> p (t d)"),
                            op0=ALU.mult, op1=ALU.add).then_inc(work_read[bank], 1)
                    elif name == "L2":
                        g, step = it - 1, stage[1]
                        if step == 0:
                            dve.wait_ge(*ring.was_read(("T1", 1)))
                            nc.vector.tensor_reduce(sum2[:], x2, axis=AX_X, op=ALU.add).then_inc(ln2_step, 1)
                        elif step <= 5:
                            dve.wait_ge(ln2_step, g * 5 + step)
                        if step == 1:
                            ts(mean2[:], sum2[:], 1.0 / D, None, ALU.mult).then_inc(ln2_step, 1)
                        elif step == 2:
                            tt(xc2, x2, bc(mean2[:]), ALU.subtract).then_inc(ln2_step, 1)
                        elif step == 3:
                            tt(hn, xc2, xc2, ALU.mult).then_inc(ln2_step, 1)
                        elif step == 4:
                            nc.vector.tensor_reduce(sum2[:], hn, axis=AX_X, op=ALU.add).then_inc(ln2_step, 1)
                        elif step == 5:
                            ts(var2[:], sum2[:], 1.0 / D, EPS, ALU.mult, ALU.add).then_inc(var2_ready, 1)
                        elif step == 6:
                            dve.wait_ge(rstd2_ready, it)
                            stt(out=hn, in0=xc2, scalar=0.0, in1=bc(rstd2[:]), op0=ALU.max,
                                op1=ALU.mult).then_inc(hn_ready, 1)
                    elif name in ("Q", "K"):
                        half, bank = stage[1], ring.bank(stage)
                        hi, lo, hi_ready = {"Q": (q_hi, q_lo, q_hi_ready), "K": (k_hi, k_lo, k_hi_ready)}[name]
                        cols = slice(half * HALF, (half + 1) * HALF)
                        dve.wait_ge(hi_ready, (it - 1) * 2 + (half + 1))
                        tt(lo[:, cols], work_ps[:, bank, :], hi[:, cols].bitcast(F32), ALU.subtract).then_inc(work_read[bank], 1)
                    elif name == "max":
                        n = stage[1]
                        if n >= 2:
                            dve.wait_ge(exp_ready, (it - 1) * NPART + (n - 1))
                        dve.wait_ge(*ring.written(("S", n)))
                        nc.vector.memset(wait_carrier[:, n:n + 1], 0.0)
                        bank = ring.bank(("S", n))
                        for hh in range(2):
                            last = nc.vector.tensor_tensor_reduce(
                                out=masked[:, n % 2, hh, :], in0=work_ps[:, bank, hh * T:(hh + 1) * T],
                                in1=mask[:, n // 2 % 2, :], scale=1.0, scalar=BIGGEST, op0=ALU.add, op1=ALU.min,
                                accum_out=neg_max[:, 2 * n + hh:2 * n + hh + 1])
                        last.then_inc(work_read[bank], 1)
                    elif name == "out":
                        r, g = stage[1], it - 1
                        n = (r + 1) * (NPART // 2) - 1
                        dve.wait_ge(exp_ready, g * NPART + (n + 1))
                        nc.vector.reciprocal(prob_rec[:], prob_sum[:, r * NPART:(r + 1) * NPART]).then_inc(rec_ready, 1)
                        dve.wait_ge(rec_ready, g * 2 + (r + 1))
                        dve.wait_ge(av_done, g * NPART + (n + 1))
                        if r == 0:
                            dve.wait_ge(stored, it * 16)
                        ys = y[:, 4 * r:4 * r + 4, :]
                        tt(ys.rearrange("p t (h d) -> p (t h) d", d=HD), av_ps[:].rearrange("p (a d) -> p a d", d=HD),
                           prob_rec[:].unsqueeze(2).to_broadcast([P, NPART, HD]), ALU.mult).then_inc(av_read, 1)
                        dve.wait_ge(av_read, g * 2 + (r + 1))
                        tt(ys, ys, x2[:, 4 * r:4 * r + 4, :], ALU.add).then_inc(y_ready, 1)

            run(dve, iteration)


INPUTS = ["x", "adj", "L0_gnn_Wg0", "L0_gnn_bg0", "L0_gnn_Wg1", "L0_gnn_bg1", "L0_gnn_Wih", "L0_gnn_Whh",
          "L0_gnn_bih", "L0_gnn_bhh", "L1_gnn_W"]


def kernel(**inputs):
    import numpy as np
    import concourse.bacc as bacc
    from concourse.bass_utils import run_bass_kernel_spmd

    nc = bacc.Bacc("TRN2", target_bir_lowering=False, num_devices=1)
    arrays, args = {}, []
    for name in INPUTS:
        a = np.ascontiguousarray(inputs[name])
        arrays[f"in_{name}"] = a
        args.append(nc.dram_tensor(f"in_{name}", a.shape, mybir.dt.from_np(a.dtype), kind="ExternalInput").ap())
    args.append(nc.dram_tensor("out", (B, T, D), F32, kind="ExternalOutput").ap())
    graph_block(nc, *args)
    r = run_bass_kernel_spmd(nc, [arrays], core_ids=[0])
    return r.results[0]["out"]
```
